# Optimizing a Trainium2 kernel written in Bass

```python
import numpy as np
import jax
import jax.numpy as jnp

def _softmax(x, axis=-1):
    return jax.nn.softmax(x, axis=axis)

def _gelu(x):
    return jax.nn.gelu(x, approximate=True)

def _silu(x):
    return jax.nn.silu(x)

def _sigmoid(x):
    return jax.nn.sigmoid(x)

def _layernorm(x, axis=-1, eps=1e-05):
    m = jnp.mean(x, axis=axis, keepdims=True)
    v = jnp.var(x, axis=axis, keepdims=True)
    return (x - m) / jnp.sqrt(v + eps)

def _scatter_add(tgt, idx, src, axis=0):
    return tgt.at[idx].add(src)

def _segment_sum(src, seg, n):
    return jax.ops.segment_sum(src, seg, n)
kernel_name = 'mk_adj_resnorm_d1_adj_r2_4fba0b'

def setup_inputs(seed: int=0):
    np.random.seed(seed)
    _w = jnp.asarray

    def _rec_inputs():
        import jax
        import jax.numpy as jnp
        _gk = jax.random.key(seed)
        x = -0.001547 + 1.001 * jax.random.normal(jax.random.fold_in(_gk, 1), (2048, 64), jnp.float32)
        _w = (1.0 + jnp.arange(2048, dtype=jnp.float32)) ** (-0.5)
        _w = _w / _w.mean()
        _pij = jnp.clip(0.000976562 * _w[:, None] * _w[None, :], 0.0, 1.0)
        _a = jax.random.uniform(jax.random.fold_in(_gk, 2), (2048, 2048)) < _pij
        _a = jnp.logical_or(_a, jnp.eye(2048, dtype=bool))
        _af = _a.astype(jnp.float32)
        _af = _af * jax.random.uniform(jax.random.fold_in(_gk, 3), (2048, 2048), jnp.float32, 0.05, 1)
        adj = _af
        return (x, adj)
    x, adj = _rec_inputs()

    def _L0_gnn_setup():
        import jax, jax.numpy as jnp
        import numpy as np

        def _laplacian(A):
            d = jnp.sum(A, axis=-1)
            dinv = 1.0 / jnp.sqrt(d)
            return A * dinv[:, None] * dinv[None, :]

        def _poly(A, theta):
            t = jax.nn.sigmoid(theta)
            N = A.shape[-1]
            P = jnp.eye(N, dtype=A.dtype)
            seg = P
            for i in range(theta.shape[0]):
                seg = seg @ A
                P = P + seg * t[i]
            return P
        key = jax.random.key(seed)
        k1, k2, k3, k4 = jax.random.split(key, 4)
        N, DIN, DOUT, K_CHEB = (2048, 64, 64, 2)
        return {'x': jax.random.normal(k1, (N, DIN), dtype=jnp.float32), 'A': jax.random.uniform(k2, (N, N), dtype=jnp.float32), 'theta': jax.random.normal(k3, (K_CHEB,), dtype=jnp.float32), 'W': jax.random.normal(k4, (DOUT, DIN), dtype=jnp.float32) / np.float32(np.sqrt(DIN)), 'b': jnp.zeros((DOUT,), dtype=jnp.float32), 'k': 4}
    _L0_gnn_all = _L0_gnn_setup()
    _L0_gnn_in = {k: v for k, v in _L0_gnn_all.items() if k in ('theta', 'W', 'b')}
    del _L0_gnn_all
    return {'x': x, 'adj': adj, 'L0_gnn_theta': _L0_gnn_in['theta'], 'L0_gnn_W': _L0_gnn_in['W'], 'L0_gnn_b': _L0_gnn_in['b']}

def reference(x, adj, L0_gnn_theta, L0_gnn_W, L0_gnn_b):
    import jax
    import jax.numpy as jnp

    def _L0_gnn_ref(x, A, theta, W, b, k):
        import jax, jax.numpy as jnp
        import numpy as np

        def _laplacian(A):
            d = jnp.sum(A, axis=-1)
            dinv = 1.0 / jnp.sqrt(d)
            return A * dinv[:, None] * dinv[None, :]

        def _poly(A, theta):
            t = jax.nn.sigmoid(theta)
            N = A.shape[-1]
            P = jnp.eye(N, dtype=A.dtype)
            seg = P
            for i in range(theta.shape[0]):
                seg = seg @ A
                P = P + seg * t[i]
            return P
        S = _laplacian(A)
        S = _poly(S, theta)
        S = _laplacian(S)
        rank = jnp.argsort(jnp.argsort(-S, axis=-1), axis=-1)
        mask = jnp.where(rank < k, jnp.float32(1.0), jnp.float32(0.0))
        S = S * mask
        x = S @ x
        return x @ W.T + b
    x = _layernorm(x + _L0_gnn_ref(x, adj, L0_gnn_theta, L0_gnn_W, L0_gnn_b, 4), axis=-1)
    return x

_drawn_inputs = setup_inputs


def setup_inputs(seed=0):
    import zlib

    import numpy as np

    out = dict(_drawn_inputs(seed))
    spreads = {'L0_gnn_b': (0.0, 0.1)}
    factors = {'L0_gnn_theta': 64.0}
    for name, (base, spread) in spreads.items():
        noise = np.random.default_rng([zlib.crc32(name.encode()), seed]).standard_normal(out[name].shape)
        drawn = base * np.exp(spread * noise) if base else spread * noise
        out[name] = jnp.asarray(drawn.astype(out[name].dtype))
    for name, factor in factors.items():
        out[name] = (out[name] * factor).astype(out[name].dtype)
    return out
```

```python
import concourse.bass as bass
from concourse import mybir
from contextlib import ExitStack


def adjacency_resnorm(nc, x, adj, theta, W, b, out):
    fp32 = mybir.dt.float32
    fp16 = mybir.dt.float16
    bf16 = mybir.dt.bfloat16
    u32 = mybir.dt.uint32
    ALU = mybir.AluOpType
    ACT = mybir.ActivationFunctionType
    AX = mybir.AxisListType

    P = 128
    N = adj.shape[0]
    D = x.shape[1]
    T = N // P
    BANK = 512
    NB = N // BANK
    TOPK = 4
    EPS = 1e-5
    LISTS = 2
    SLOTS = LISTS * P
    HALF = T // 2
    LOOK = 3
    AT_RING = 4
    PICKS = 4
    AHEAD = 4
    DIAG = 384

    with ExitStack() as ctx:
        def sb(name, shape, dt=fp32):
            return ctx.enter_context(nc.sbuf_tensor(name, shape, dt))

        def sem(name):
            return ctx.enter_context(nc.semaphore(name))

        at_dram = nc.dram_tensor("at_dram", [T * N + 1, P], fp32, kind="Internal").ap()
        at_tiles = at_dram[0:T * N, :].rearrange("(t p j) i -> t p j i", t=T, j=T)
        xw_dram = nc.dram_tensor("xw_dram", [N, D], fp32, kind="Internal").ap()
        w_dram = nc.dram_tensor("w_dram", [N, 1], fp32, kind="Internal").ap()
        vec_dram = [nc.dram_tensor(f"vec_dram{n}", [P, T], fp32, kind="Internal").ap() for n in range(3)]

        A = sb("A", [P, T, N])
        big = [sb(f"big{n}", [P, N]) for n in range(6)]
        stage = big[0:2]
        at_stage = [big[2 + n][:, :].rearrange("p (j i) -> p j i", j=T) for n in range(AT_RING)]
        rows = [big[0:2], big[2:4]]
        G = big[4:6]
        all_edges = [big[2 * s][:, :].rearrange("p (j i) -> p j i", j=T) for s in range(2)]
        vec = sb("vec", [P, N])
        junk = sb("junk", [P, N], bf16)
        ident = sb("ident", [P, P])
        t0_ident = sb("t0_ident", [P, P])
        ones = sb("ones", [P, P])
        my_slot = sb("my_slot", [P, 2 * T])
        tile_base = sb("tile_base", [P, 2 * T])
        tile_row = sb("tile_row", [P, 2 * T])
        part_no = sb("part_no", [P, 1])
        par4 = sb("par4", [P, 2, 4])
        parity = sb("parity", [P, 2])
        count = sb("count", [P, 2])
        prefix = sb("prefix", [P, 2, P + LOOK], fp16)
        start = sb("start", [P, 2])
        end = sb("end", [P, 2])
        over = sb("over", [P, 2])
        over_sum = sb("over_sum", [P, 1])
        flag = sb("flag", [P, 1], u32)
        looked = sb("looked", [P, 2 * T, LOOK])
        local = sb("local", [P, 2 * T])
        signs = sb("signs", [P, 2 * T])
        node = sb("node", [P, 2 * T])
        node_at = sb("node_at", [P, 2 * T])
        lists = sb("lists", [P, T, 2, LISTS], u32)
        list_now = [sb(f"list_now{s}", [P, 2, LISTS], u32) for s in range(2)]
        t01 = sb("t01", [P, 2])
        d = sb("d", [P, T])
        root = sb("root", [P, T])
        y = sb("y", [P, T])
        tmp = sb("tmp", [P, T])
        tmp2 = sb("tmp2", [P, T])
        y2 = sb("y2", [P, T])
        w = sb("w", [P, T])
        r1 = sb("r1", [P, T])
        v = sb("v", [P, T])
        r2 = sb("r2", [P, T])
        d2 = sb("d2", [P, T])
        c = sb("c", [P, T])
        dc = sb("dc", [P, T])
        hs = sb("hs", [P, T, D])
        Ws = sb("Ws", [D, D])
        WT = sb("WT", [D, D])
        b_all = sb("b_all", [P, D])
        edge = [sb(f"edge{s}", [P, LISTS, P]) for s in range(2)]
        edge_w = [sb(f"edge_w{s}", [P, LISTS]) for s in range(2)]
        own_raw = [sb(f"own_raw{s}", [P, P]) for s in range(2)]
        own = [sb(f"own{s}", [P, P]) for s in range(2)]
        top = [sb(f"top{s}", [P, 8]) for s in range(PICKS)]
        idx = [sb(f"idx{s}", [P, 8], u32) for s in range(PICKS)]
        coef = [sb(f"coef{s}", [P, 8]) for s in range(PICKS)]
        picked = [sb(f"picked{s}", [P, TOPK, D]) for s in range(PICKS)]
        mean = sb("mean", [P, T])
        var = sb("var", [P, T])
        std = sb("std", [P, T])
        rstd = sb("rstd", [P, T])
        xT = big[5][0:D, :].rearrange("f (t p) -> f t p", t=T)
        xw = vec[:, 0:T * D].rearrange("p (t f) -> p t f", t=T)
        not_own = picked[0][:, :, :].rearrange("p m f -> p (m f)").rearrange("p (t j) -> p t j", t=T)
        before = picked[1][:, 0:2, :].rearrange("p m f -> p (m f)")
        slot_no = picked[2][:, :, :].rearrange("p m f -> p (m f)")
        zero_row = own[0][0:1, :]
        mask = big[0][:, 0:T * T].rearrange("p (t j) -> p t j", t=T)
        past = big[0][:, BANK:BANK + 2 * SLOTS].rearrange("p (h s) -> p h s", h=2)
        inside = big[0][:, 2 * BANK:2 * BANK + 2 * SLOTS].rearrange("p (h s) -> p h s", h=2)
        pick_block = big[1][:, 0:2 * SLOTS].bitcast(fp16).rearrange("p (h r s) -> p h r s", h=2, r=2)
        sq = big[0][:, 0:T * D].rearrange("p (t f) -> p t f", t=T)

        ps = [ctx.enter_context(nc.psum_tensor(f"ps{s}", [P, N], fp32)) for s in range(2)]

        small_in = sem("small_in")
        consts = sem("consts")
        making = sem("making")
        t01_ready = sem("t01_ready")
        d2_ready = sem("d2_ready")
        x_turned = sem("x_turned")
        x_turned_out = sem("x_turned_out")
        xw_made = sem("xw_made")
        xw_out = sem("xw_out")
        xw_stored = sem("xw_stored")
        zero_stored = sem("zero_stored")
        loaded = [sem(f"loaded{s}") for s in range(2)]
        resident = sem("resident")
        turned = sem("turned")
        turned_out = sem("turned_out")
        col_summed = sem("col_summed")
        at_stored = [sem(f"at_stored{s}") for s in range(AT_RING)]
        rooted = sem("rooted")
        step = sem("step")
        col_ready = sem("col_ready")
        w_ready = sem("w_ready")
        w_stored = sem("w_stored")
        vec_stored = [sem(f"vec_stored{n}") for n in range(3)]
        vec_spread = [sem(f"vec_spread{n}") for n in range(3)]
        mask_ready = sem("mask_ready")
        mask_turned = sem("mask_turned")
        prefix_ready = sem("prefix_ready")
        start_made = sem("start_made")
        over_ready = sem("over_ready")
        over_made = sem("over_made")
        flag_ready = sem("flag_ready")
        blocks_ready = sem("blocks_ready")
        looked_made = sem("looked_made")
        prefix_made = sem("prefix_made")
        local_ready = sem("local_ready")
        counted = sem("counted")
        lists_ready = sem("lists_ready")
        list_taken = sem("list_taken")
        edges_in = [sem(f"edges_in{s}") for s in range(2)]
        edge_w_in = [sem(f"edge_w_in{s}") for s in range(2)]
        rows_in = [[sem(f"rows_in{s}{q}") for q in range(LISTS)] for s in range(2)]
        own_in = [sem(f"own_in{s}") for s in range(2)]
        edges_ready = sem("edges_ready")
        all_in = [sem(f"all_in{s}") for s in range(2)]
        all_scaled = sem("all_scaled")
        all_ready = sem("all_ready")
        own_scaled = sem("own_scaled")
        own_ready = sem("own_ready")
        b_made = sem("b_made")
        b_out = sem("b_out")
        pass1 = sem("pass1")
        pass2 = sem("pass2")
        g_scaled = sem("g_scaled")
        g_ready = sem("g_ready")
        top_ready = sem("top_ready")
        idx_ready = sem("idx_ready")
        coef_ready = sem("coef_ready")
        picks_in = [sem(f"picks_in{s}") for s in range(PICKS)]
        weighted = sem("weighted")
        pairs = sem("pairs")
        summed = sem("summed")
        hs_ready = sem("hs_ready")
        ln_var = sem("ln_var")
        ln_root = sem("ln_root")
        finished = sem("finished")
        out_stored = sem("out_stored")

        def tile_of(buffer3, t):
            return buffer3[:, bass.ds(t, 1), :].rearrange("p o f -> p (o f)")

        def overflow_flag(engine):
            engine.wait_ge(flag_ready, 1)
            return engine.value_load(flag[0:1, 0:1])

        block = ctx.enter_context(nc.Block())

        @block.sync
        def _(sp):
            adj_tiles = adj.rearrange("(p t) k -> t p k", t=T)
            for s in range(2):
                sp.dma_start(stage[s][:, :], adj_tiles[s]).then_inc(loaded[s], 16)
            with sp.Fori(1, T // 2) as i:
                for s in range(2):
                    sp.wait_ge(resident, 2 * i + s - 1)
                    sp.wait_ge(col_summed, 2 * i + s - 1)
                    sp.dma_start(stage[s][:, :], adj_tiles[bass.ds(2 * i + s, 1)].rearrange("o p k -> p (o k)")).then_inc(loaded[s], 16)
            sp.wait_ge(col_ready, 1)
            sp.wait_ge(xw_stored, 16)
            sp.dma_start(vec_dram[0], y[:, :]).then_inc(vec_stored[0], 16)
            sp.wait_ge(vec_stored[0], 16)
            sp.dma_start(vec[:, :], vec_dram[0].rearrange("p t -> (p t)").rearrange("(o k) -> o k", o=1).to_broadcast([P, N])).then_inc(vec_spread[0], 16)
            sp.wait_ge(w_ready, 1)
            sp.dma_start(w_dram.rearrange("(p t) o -> p (t o)", t=T), w[:, :]).then_inc(w_stored, 16)

            for s in range(AT_RING):
                sp.wait_ge(at_stored[s], 16 * (T // AT_RING))

            def spread(n, vector):
                sp.wait_ge(col_ready, n + 1)
                sp.dma_start(vec_dram[n], vector[:, :]).then_inc(vec_stored[n], 16)
                sp.wait_ge(vec_stored[n], 16)
                sp.dma_start(vec[:, :], vec_dram[n].rearrange("p t -> (p t)").rearrange("(o k) -> o k", o=1).to_broadcast([P, N])).then_inc(vec_spread[n], 16)

            def own_rows(s, t):
                sp.dma_start(own_raw[s][:, :], at_tiles[bass.ds(t, 1), :, bass.ds(t, 1), :].rearrange("a p b i -> p (a b i)")).then_inc(own_in[s], 16)

            def all_rows(s, t):
                sp.dma_start(all_edges[s], at_tiles[bass.ds(t, 1)].rearrange("o p j i -> p (o j) i")).then_inc(all_in[s], 16)

            overflow = overflow_flag(sp)
            with sp.If(overflow == 0):
                for s in range(2):
                    own_rows(s, s)
                for s in range(2):
                    sp.wait_ge(own_ready, s + 1)
                    own_rows(s, s + 2)
                spread(1, v)
                spread(2, c)
                with sp.Fori(2, T // 2) as i:
                    for s in range(2):
                        sp.wait_ge(own_ready, 2 * i + s - 1)
                        own_rows(s, 2 * i + s)
            with sp.Else():
                sp.wait_ge(lists_ready, 1)
                sp.wait_ge(counted, 2 * T)
                sp.wait_ge(resident, T)
                sp.wait_ge(col_summed, T)
                for s in range(2):
                    all_rows(s, s)
                spread(1, v)
                spread(2, c)
                with sp.Fori(1, T // 2) as i:
                    for s in range(2):
                        sp.wait_ge(b_made, 2 * i + s - 1)
                        all_rows(s, 2 * i + s)
            sp.wait_ge(finished, 1)
            sp.dma_start(out.rearrange("(p t) f -> p t f", t=T), hs[:, :, :]).then_inc(out_stored, 16)
            sp.wait_ge(out_stored, 16)

        @block.scalar
        def _(act):
            act.dma_start(hs[:, :, :], x.rearrange("(p t) f -> p t f", t=T)).then_inc(small_in, 16)
            act.dma_start(Ws[:, :], W).then_inc(small_in, 16)
            act.dma_start(t01[:, :], theta.rearrange("(o k) -> o k", o=1).to_broadcast([P, 2])).then_inc(small_in, 16)
            act.dma_start(b_all[:, :], b.rearrange("(o k) -> o k", o=1).to_broadcast([P, D])).then_inc(small_in, 16)
            act.wait_ge(small_in, 64)
            nc.scalar.activation(t01[:, :], t01[:, :], ACT.Sigmoid).then_inc(t01_ready, 1)
            with act.Fori(0, T // 2) as i:
                for s in range(2):
                    act.wait_ge(loaded[s], 16 * i + 16)
                    nc.scalar.activation(tile_of(A, 2 * i + s), stage[s][:, :], ACT.Copy,
                                         accum_out=d[:, bass.ds(2 * i + s, 1)]).then_inc(resident, 1)
            act.wait_ge(resident, T)
            nc.scalar.activation(root[:, :], d[:, :], ACT.Sqrt).then_inc(rooted, 1)
            act.wait_ge(local_ready, 1)
            for h in range(2):
                act.wait_ge(prefix_made, h + 1)
                with act.Fori(0, T) as n:
                    nc.scalar.activation(junk[:, bass.ds(n * P, P)], ps[0][:, bass.ds(n * P, P)], ACT.Sign, scale=-1.0,
                                         bias=local[:, bass.ds(n + h * T, 1)],
                                         accum_out=signs[:, bass.ds(n + h * T, 1)]).then_inc(counted, 1)
                if h == 0:
                    act.wait_ge(counted, T)

            def edges(s, n, t):
                act.wait_ge(own_in[s], 16 * n + 16)
                nc.scalar.activation(own_raw[s][:, :], own_raw[s][:, :], ACT.Copy,
                                     scale=w[:, bass.ds(t, 1)]).then_inc(own_scaled, 1)
                act.wait_ge(edges_in[s], 32 * n + 32)
                act.wait_ge(edge_w_in[s], 32 * n + 32)
                for q in range(LISTS):
                    last = nc.scalar.activation(edge[s][:, q, :], edge[s][:, q, :], ACT.Copy, scale=edge_w[s][:, q:q + 1])
                last.then_inc(edges_ready, 1)

            def take_b(s, t):
                act.wait_ge(b_made, t + 1)
                if not (isinstance(t, int) and t < 2):
                    act.wait_ge(idx_ready, t - 1)
                nc.scalar.activation(G[s][:, :], ps[s][:, :], ACT.Copy).then_inc(b_out, 1)

            def root_d2():
                act.wait_ge(d2_ready, 1)
                nc.scalar.activation(root[:, :], d2[:, :], ACT.Sqrt).then_inc(rooted, 1)

            overflow = overflow_flag(act)
            with act.If(overflow == 0):
                edges(0, 0, 0)
                edges(1, 0, 1)
                take_b(0, 0)
                edges(0, 1, 2)
                take_b(1, 1)
                edges(1, 1, 3)
                root_d2()
                with act.Fori(1, T // 2 - 1) as i:
                    for s in range(2):
                        take_b(s, 2 * i + s)
                        edges(s, i + 1, 2 * i + s + 2)
                take_b(0, T - 2)
                take_b(1, T - 1)
            with act.Else():
                take_b(0, 0)
                take_b(1, 1)
                root_d2()
                with act.Fori(1, T // 2) as i:
                    for s in range(2):
                        take_b(s, 2 * i + s)
            act.wait_ge(ln_var, 1)
            nc.scalar.activation(std[:, :], var[:, :], ACT.Sqrt).then_inc(ln_root, 1)

        @block.tensor
        def _(pe):
            pe.wait_ge(consts, 1)
            pe.wait_ge(small_in, 64)
            for t in range(T):
                nc.tensor.transpose(ps[0][0:D, t * P:(t + 1) * P], hs[:, t, :], ident[:, :])
            nc.tensor.transpose(ps[1][0:D, 0:D], Ws[:, :], ident[0:D, 0:D]).then_inc(x_turned, 1)
            pe.wait_ge(x_turned_out, 1)
            for t in range(T):
                mm = nc.tensor.matmul(ps[1][:, t * D:(t + 1) * D], xT[:, t, :], WT[:, :], start=True, stop=True)
            mm.then_inc(xw_made, 1)
            pe.wait_ge(xw_out, 1)
            def turn(s, i):
                pe.wait_ge(loaded[s], 16 * i + 16)
                for h in range(2):
                    if not (isinstance(i, int) and 2 * s + h < 2):
                        pe.wait_ge(turned_out, 4 * i + max(0, 2 * s + h - 1))
                    half = ps[0][:, h * 2 * BANK:(h + 1) * 2 * BANK]
                    for j in range(HALF):
                        mm = nc.tensor.transpose(half[:, j * P:(j + 1) * P], stage[s][:, h * HALF + j:N:T], ident[:, :])
                    mm.then_inc(turned, 1)
                for j in range(T):
                    mm = nc.tensor.matmul(ps[1][:, bass.ds((2 * i + s) * T + j, 1)], stage[s][:, j:N:T], ones[:, 0:1],
                                          start=True, stop=True, skip_group_check=True)
                mm.then_inc(col_summed, 1)

            turn(0, 0)
            turn(1, 0)
            with pe.Fori(1, T // 2) as i:
                for s in range(2):
                    turn(s, i)
            pe.wait_ge(mask_ready, 1)
            for h in range(2):
                mm = nc.tensor.transpose(ps[1][:, BANK + h * P:BANK + (h + 1) * P],
                                         mask[:, h * HALF:(h + 1) * HALF, :].rearrange("p t j -> p (t j)"), ident[:, :])
            mm.then_inc(mask_turned, 1)
            pe.wait_ge(prefix_ready, 1)
            nc.tensor.matmul(ps[1][:, 2 * BANK:2 * BANK + 2], before, count[:, :], start=True, stop=True).then_inc(start_made, 1)
            pe.wait_ge(over_ready, 1)
            nc.tensor.matmul(ps[1][:, 2 * BANK + 8:2 * BANK + 10], ones[:, :], over[:, :], start=True, stop=True).then_inc(over_made, 1)
            pe.wait_ge(blocks_ready, 1)
            pe.wait_ge(flag_ready, 1)
            for t in range(T):
                h, g, r = t // HALF, (t % HALF) // 2, t % 2
                k = slice(32 * g, 32 * g + 32)
                for q in range(LISTS):
                    at = g * BANK + DIAG + ((h * 2 + r) * LISTS + q) * LOOK
                    mm = nc.tensor.matmul(ps[1][:, at:at + LOOK], pick_block[k, h, r, q * P:(q + 1) * P],
                                          prefix[k, h, P:P + LOOK], start=True, stop=True, skip_group_check=True)
            mm.then_inc(looked_made, 1)
            for h in range(2):
                if h == 1:
                    pe.wait_ge(counted, T)
                else:
                    pe.wait_ge(turned_out, 2 * T)
                for t in range(HALF):
                    g, r = t // 2, t % 2
                    k = slice(32 * g, 32 * g + 32)
                    for q in range(LISTS):
                        at = (t * LISTS + q) * P
                        mm = nc.tensor.matmul(ps[0][:, at:at + P], pick_block[k, h, r, q * P:(q + 1) * P],
                                              prefix[k, h, 0:P], start=True, stop=True, skip_group_check=True)
                mm.then_inc(prefix_made, 1)

            def product(s, n, t):
                pe.wait_ge(own_ready, t + 1)
                pe.wait_ge(edges_ready, t + 1)
                if isinstance(t, int):
                    pe.wait_ge(counted, 2 * T)
                    pe.wait_ge(local_ready, 1)
                else:
                    pe.wait_ge(b_out, t - 1)
                for k in range(LISTS + 1):
                    if k:
                        pe.wait_ge(rows_in[s][k - 1], 16 * n + 16)
                    for m in range(NB):
                        cols = slice(m * BANK, (m + 1) * BANK)
                        if k:
                            mm = nc.tensor.matmul(ps[s][:, cols], edge[s][:, k - 1, :], rows[s][k - 1][:, cols],
                                                  start=False, stop=(k == LISTS), skip_group_check=True)
                        else:
                            mm = nc.tensor.matmul(ps[s][:, cols], own[s][:, :],
                                                  A[:, bass.ds(t, 1), cols].rearrange("p o k -> p (o k)"),
                                                  start=True, stop=False, skip_group_check=True)
                mm.then_inc(b_made, 1)

            def product_of_all(s, t):
                pe.wait_ge(all_ready, t + 1)
                if isinstance(t, int):
                    pe.wait_ge(counted, 2 * T)
                    pe.wait_ge(local_ready, 1)
                else:
                    pe.wait_ge(b_out, t - 1)
                for j in range(T):
                    for m in range(NB):
                        cols = slice(m * BANK, (m + 1) * BANK)
                        mm = nc.tensor.matmul(ps[s][:, cols], all_edges[s][:, j, :], A[:, j, cols],
                                              start=(j == 0), stop=(j == T - 1), skip_group_check=True)
                mm.then_inc(b_made, 1)

            overflow = overflow_flag(pe)
            with pe.If(overflow == 0):
                product(0, 0, 0)
                product(1, 0, 1)
                with pe.Fori(1, T // 2) as i:
                    for s in range(2):
                        product(s, i, 2 * i + s)
            with pe.Else():
                product_of_all(0, 0)
                product_of_all(1, 1)
                with pe.Fori(1, T // 2) as i:
                    for s in range(2):
                        product_of_all(s, 2 * i + s)

        @block.vector
        def _(dve):
            chain = [0]

            def done(ins):
                chain[0] += 1
                ins.then_inc(step, 1)
                dve.wait_ge(step, chain[0])

            dve.wait_ge(x_turned, 1)
            nc.vector.tensor_copy(xT[:, :, :], ps[0][0:D, :].rearrange("f (t p) -> f t p", t=T))
            nc.vector.tensor_copy(WT[:, :], ps[1][0:D, 0:D]).then_inc(x_turned_out, 1)
            nc.vector.tensor_tensor(hs[:, :, :], hs[:, :, :], b_all[:, None, :].to_broadcast([P, T, D]), ALU.add)
            dve.wait_ge(xw_made, 1)
            nc.vector.tensor_copy(xw, ps[1][:, 0:T * D].rearrange("p (t f) -> p t f", t=T)).then_inc(xw_out, 1)

            def take_turned(s, i):
                for h in range(2):
                    dve.wait_ge(turned, 2 * AT_RING * i + 2 * s + h + 1)
                    if h == 0 and not isinstance(i, int):
                        dve.wait_ge(at_stored[s], 16 * i)
                    nc.vector.tensor_copy(at_stage[s][:, h * HALF:(h + 1) * HALF, :],
                                          ps[0][:, h * 2 * BANK:(h + 1) * 2 * BANK].rearrange("p (j i) -> p j i", j=HALF)
                                          ).then_inc(turned_out, 1)

            for s in range(AT_RING):
                take_turned(s, 0)
            with dve.Fori(1, T // AT_RING) as i:
                for s in range(AT_RING):
                    take_turned(s, i)

            def inverse_root(dst, src):
                done(nc.vector.reciprocal(tmp[:, :], root[:, :]))
                done(nc.vector.tensor_tensor(tmp2[:, :], tmp[:, :], tmp[:, :], ALU.mult))
                done(nc.vector.tensor_tensor(tmp2[:, :], tmp2[:, :], src[:, :], ALU.mult))
                done(nc.vector.tensor_scalar(tmp2[:, :], tmp2[:, :], -0.5, 1.5, ALU.mult, ALU.add))
                done(nc.vector.tensor_tensor(dst[:, :], tmp[:, :], tmp2[:, :], ALU.mult))

            dve.wait_ge(col_summed, T)
            dve.wait_ge(consts, 2)
            dve.wait_ge(resident, T)
            nc.vector.scalar_tensor_tensor(out=mask, in0=ps[1][:, 0:T * T].rearrange("p (t j) -> p t j", t=T), scalar=0.0,
                                           in1=not_own, op0=ALU.not_equal, op1=ALU.mult).then_inc(mask_ready, 1)
            dve.wait_ge(rooted, 1)
            inverse_root(y, d)
            nc.vector.tensor_tensor(y2[:, :], y[:, :], y[:, :], ALU.mult).then_inc(col_ready, 1)
            dve.wait_ge(mask_turned, 1)
            for h in range(2):
                done(nc.vector.tensor_tensor_scan(out=prefix[:, h, 0:P], data0=ones[:, :], data1=ps[1][:, BANK + h * P:BANK + (h + 1) * P],
                                                  initial=0.0, op0=ALU.mult, op1=ALU.add))
            nc.vector.tensor_copy(count[:, :], prefix[:, :, P - 1]).then_inc(prefix_ready, 1)
            dve.wait_ge(t01_ready, 1)
            nc.vector.tensor_scalar(w[:, :], y2[:, :], t01[:, 1:2], None, ALU.mult).then_inc(w_ready, 1)
            dve.wait_ge(start_made, 1)
            done(nc.vector.tensor_copy(start[:, :], ps[1][:, 2 * BANK:2 * BANK + 2]))
            done(nc.vector.tensor_tensor(end[:, :], start[:, :], count[:, :], ALU.add))
            nc.vector.tensor_scalar(over[:, :], end[:, :], float(SLOTS), None, ALU.is_gt).then_inc(over_ready, 1)
            for h in range(2):
                nc.vector.tensor_copy(prefix[:, h, P:P + 1], start[:, h:h + 1])
                nc.vector.tensor_copy(prefix[:, h, P + 1:P + 2], part_no[:, :])
                nc.vector.memset(prefix[:, h, P + 2:P + 3], 1.0)
                done(nc.vector.tensor_scalar(past[:, h, :], slot_no, end[:, h:h + 1], None, ALU.is_ge))
                done(nc.vector.scalar_tensor_tensor(out=inside[:, h, :], in0=slot_no, scalar=start[:, h:h + 1],
                                                    in1=past[:, h, :], op0=ALU.is_ge, op1=ALU.subtract))
                for r in range(2):
                    last = nc.vector.tensor_scalar(pick_block[:, h, r, :], inside[:, h, :], parity[:, r:r + 1], None, ALU.mult)
            last.then_inc(blocks_ready, 1)
            dve.wait_ge(over_made, 1)
            done(nc.vector.tensor_reduce(over_sum[:, :], ps[1][:, 2 * BANK + 8:2 * BANK + 10], AX.X, ALU.add))
            nc.vector.tensor_copy(flag[:, :], over_sum[:, :]).then_inc(flag_ready, 1)
            dve.wait_ge(looked_made, 1)
            banks = ps[1][:, :].rearrange("p (g n) -> p g n", g=NB)[:, :, DIAG:DIAG + 4 * LISTS * LOOK]
            looked_v = looked[:, :, :].rearrange("p (h g rq) l -> p h g rq l", h=2, g=NB)
            for h in range(2):
                last = nc.vector.tensor_copy(looked_v[:, h], banks.rearrange("p g (h rq l) -> p h g rq l", h=2, l=LOOK)[:, h])
            done(last)
            done(nc.vector.tensor_tensor(local[:, :], my_slot[:, :], looked[:, :, 0], ALU.subtract))
            nc.vector.tensor_scalar(local[:, :], local[:, :], 0.5, None, ALU.add).then_inc(local_ready, 1)
            dve.wait_ge(counted, 2 * T)
            done(nc.vector.tensor_scalar(node[:, :], signs[:, :], T / 2.0, T * P / 2.0, ALU.mult, ALU.add))
            done(nc.vector.tensor_tensor(node[:, :], node[:, :], looked[:, :, 1], ALU.add))
            done(nc.vector.tensor_tensor(node[:, :], node[:, :], tile_base[:, :], ALU.subtract))
            done(nc.vector.tensor_tensor(node_at[:, :], node[:, :], tile_row[:, :], ALU.add))
            done(nc.vector.tensor_scalar(node_at[:, :], node_at[:, :], float(-T * N), None, ALU.add))
            done(nc.vector.tensor_tensor(node_at[:, :], node_at[:, :], looked[:, :, 2], ALU.mult))
            done(nc.vector.tensor_scalar(node_at[:, :], node_at[:, :], float(T * N), None, ALU.add))
            done(nc.vector.tensor_tensor(node[:, :], node[:, :], looked[:, :, 2], ALU.mult))
            nc.vector.tensor_copy(lists[:, :, 0, :], node[:, :].rearrange("p (t q) -> p t q", t=T))
            nc.vector.tensor_copy(lists[:, :, 1, :], node_at[:, :].rearrange("p (t q) -> p t q", t=T)).then_inc(lists_ready, 1)
            for n, (result, passed) in enumerate(((r1, pass1), (r2, pass2))):
                dve.wait_ge(vec_spread[n], 16)
                with dve.Fori(0, T) as t:
                    nc.vector.scalar_tensor_tensor(out=junk[:, :], in0=tile_of(A, t), scalar=1.0, in1=vec[:, :],
                                                   op0=ALU.mult, op1=ALU.mult, accum_out=result[:, bass.ds(t, 1)]).then_inc(passed, 1)
                    dve.wait_ge(passed, t + 1)
                if n == 0:
                    dve.wait_ge(pass1, T)
                    done(nc.vector.tensor_tensor(v[:, :], y2[:, :], r1[:, :], ALU.mult))
                    nc.vector.tensor_scalar(tmp[:, :], r1[:, :], t01[:, 0:1], None, ALU.mult).then_inc(col_ready, 1)
            dve.wait_ge(col_ready, 2)
            done(nc.vector.scalar_tensor_tensor(out=tmp2[:, :], in0=r2[:, :], scalar=t01[:, 1:2], in1=tmp[:, :], op0=ALU.mult, op1=ALU.add))
            done(nc.vector.tensor_tensor(tmp[:, :], tmp2[:, :], y[:, :], ALU.mult))
            done(nc.vector.tensor_scalar(d2[:, :], tmp[:, :], 1.0, None, ALU.add))
            nc.vector.tensor_copy(tmp[:, :], d2[:, :]).then_inc(d2_ready, 1)
            dve.wait_ge(rooted, 2)
            dve.wait_ge(d2_ready, 1)
            inverse_root(c, d2)
            done(nc.vector.tensor_tensor(c[:, :], c[:, :], y[:, :], ALU.mult))
            nc.vector.tensor_tensor(dc[:, :], c[:, :], d[:, :], ALU.mult).then_inc(col_ready, 1)
            dve.wait_ge(vec_spread[2], 16)
            dve.wait_ge(col_ready, 3)

            def scale(s, t):
                dve.wait_ge(b_out, t + 1)
                nc.vector.tensor_tensor(G[s][:, :], G[s][:, :], vec[:, :], ALU.mult).then_inc(g_scaled, 1)
                dve.wait_ge(g_scaled, t + 1)
                diagonal = G[s][:, :].rearrange("p (k o) -> p k o", o=T)[:, :, bass.ds(t, 1)].rearrange("p k o -> p (k o)")
                nc.vector.scalar_tensor_tensor(out=diagonal, in0=ident[:, :], scalar=dc[:, bass.ds(t, 1)], in1=diagonal,
                                               op0=ALU.mult, op1=ALU.add).then_inc(g_ready, 1)

            def find(s, r, t):
                nc.vector.max(out=top[r][:, :], in_=G[s][:, :]).then_inc(top_ready, 1)
                dve.wait_ge(top_ready, t + 1)
                nc.vector.tensor_scalar(coef[r][:, :], top[r][:, :], c[:, bass.ds(t, 1)], None, ALU.mult).then_inc(coef_ready, 1)
                nc.vector.max_index(out=idx[r][:, :], in_max=top[r][:, :], in_values=G[s][:, :]).then_inc(idx_ready, 1)

            def add_picked(r, n, t, g_tile=None):
                dve.wait_ge(picks_in[r], 16 * TOPK * (n + 1))
                dve.wait_ge(coef_ready, t + 1)
                if g_tile is not None:
                    dve.wait_ge(g_ready, g_tile + 1)
                nc.vector.tensor_tensor(picked[r][:, :, :], picked[r][:, :, :], coef[r][:, 0:TOPK, None].to_broadcast([P, TOPK, D]),
                                        ALU.mult).then_inc(weighted, 1)
                dve.wait_ge(weighted, t + 1)
                nc.vector.tensor_tensor(picked[r][:, 0:2, :], picked[r][:, 0:2, :], picked[r][:, 2:4, :], ALU.add).then_inc(pairs, 1)
                dve.wait_ge(pairs, t + 1)
                nc.vector.tensor_tensor(picked[r][:, 0, :], picked[r][:, 0, :], picked[r][:, 1, :], ALU.add).then_inc(summed, 1)
                dve.wait_ge(summed, t + 1)
                nc.vector.tensor_tensor(tile_of(hs, t), tile_of(hs, t), picked[r][:, 0, :], ALU.add).then_inc(hs_ready, 1)

            for t in range(2):
                scale(t, t)
                dve.wait_ge(g_ready, t + 1)
                find(t, t, t)
            with dve.Fori(0, (T - 4) // PICKS) as i:
                for j in range(PICKS):
                    scale(j % 2, 4 * i + j + 2)
                    add_picked(j, i, 4 * i + j, 4 * i + j + 2)
                    find(j % 2, (j + 2) % PICKS, 4 * i + j + 2)
            for t in range(T - 2, T):
                scale(t % 2, t)
                add_picked((t - 2) % PICKS, (t - 2) // PICKS, t - 2, t)
                find(t % 2, t % PICKS, t)
            for t in range(T - 2, T):
                add_picked(t % PICKS, t // PICKS, t)
            dve.wait_ge(hs_ready, T)
            done(nc.vector.tensor_reduce(mean[:, :], hs[:, :, :], AX.X, ALU.add))
            done(nc.vector.tensor_scalar(mean[:, :], mean[:, :], 1.0 / D, None, ALU.mult))
            done(nc.vector.tensor_tensor(hs[:, :, :], hs[:, :, :], mean[:, :, None].to_broadcast([P, T, D]), ALU.subtract))
            done(nc.vector.tensor_tensor(sq, hs[:, :, :], hs[:, :, :], ALU.mult))
            done(nc.vector.tensor_reduce(var[:, :], sq, AX.X, ALU.add))
            nc.vector.tensor_scalar(var[:, :], var[:, :], 1.0 / D, EPS, ALU.mult, ALU.add).then_inc(ln_var, 1)
            dve.wait_ge(ln_root, 1)
            done(nc.vector.reciprocal(rstd[:, :], std[:, :]))
            nc.vector.tensor_tensor(hs[:, :, :], hs[:, :, :], rstd[:, :, None].to_broadcast([P, T, D]), ALU.mult).then_inc(finished, 1)

        @block.gpsimd
        def _(pool):
            made = [0]

            def const(ins):
                made[0] += 1
                ins.then_inc(making, 1)
                pool.wait_ge(making, made[0])

            def keep(buffer, pattern, base, per_partition, compare=ALU.is_ge):
                const(nc.gpsimd.affine_select(out=buffer, in_=buffer, compare_op=compare, fill=0.0, base=base,
                                              pattern=pattern, channel_multiplier=per_partition))

            const(nc.gpsimd.memset(ones[:, :], 1.0))
            nc.gpsimd.affine_select(out=ident[:, :], in_=ones[:, :], compare_op=ALU.is_equal, fill=0.0, base=0,
                                    pattern=[[-1, P]], channel_multiplier=1).then_inc(consts, 1)
            const(nc.gpsimd.memset(not_own, 1.0))
            keep(not_own, [[1, T], [-1, T]], 0, 0, ALU.not_equal)
            const(nc.gpsimd.memset(before, 1.0))
            keep(before, [[1, P]], -1, -1)
            keep(before, [[-T, HALF], [0, T]], 0, 1)
            const(nc.gpsimd.memset(par4[:, :, :], 1.0))
            keep(par4[:, :, :], [[-T, 2], [-2 * T, 4]], 0, 1)
            keep(par4[:, :, :], [[T, 2], [2 * T, 4]], T - 1, -1)
            const(nc.gpsimd.tensor_tensor(par4[:, :, 0:2], par4[:, :, 0:2], par4[:, :, 2:4], ALU.add))
            const(nc.gpsimd.tensor_tensor(parity[:, :], par4[:, :, 0], par4[:, :, 1], ALU.add))
            exact = dict(allow_small_or_imprecise_dtypes=True)
            const(nc.gpsimd.iota(slot_no, [[1, SLOTS]], base=0, channel_multiplier=0, **exact))
            const(nc.gpsimd.iota(my_slot[:, :], [[0, T], [P, LISTS]], base=0, channel_multiplier=1, **exact))
            const(nc.gpsimd.iota(tile_base[:, :], [[0, 2], [T, HALF], [0, LISTS]], base=0, channel_multiplier=0, **exact))
            const(nc.gpsimd.iota(tile_row[:, :], [[N, T], [0, LISTS]], base=0, channel_multiplier=0, **exact))
            const(nc.gpsimd.memset(zero_row, 0.0))
            nc.gpsimd.iota(part_no[:, :], [[0, 1]], base=0, channel_multiplier=1, **exact).then_inc(consts, 1)
            pool.dma_start(at_dram[T * N:T * N + 1, :], zero_row).then_inc(zero_stored, 16)
            pool.wait_ge(xw_out, 1)
            pool.dma_start(xw_dram.rearrange("(p t) f -> p t f", t=T), xw).then_inc(xw_stored, 16)
            with pool.Fori(0, T // AT_RING) as i:
                for s in range(AT_RING):
                    pool.wait_ge(turned_out, 2 * AT_RING * i + 2 * s + 2)
                    pool.dma_start(at_tiles[bass.ds(AT_RING * i + s, 1)].rearrange("o p j i -> p (o j) i"),
                                   at_stage[s]).then_inc(at_stored[s], 16)
            pool.wait_ge(t01_ready, 1)
            nc.gpsimd.tensor_tensor(t0_ident[:, :], ident[:, :], t01[:, 0:1].to_broadcast([P, P]), ALU.mult).then_inc(making, 1)
            pool.wait_ge(making, made[0] + 1)
            for s in range(AT_RING):
                pool.wait_ge(at_stored[s], 16 * (T // AT_RING))
            pool.wait_ge(w_stored, 16)
            pool.wait_ge(resident, T)
            pool.wait_ge(col_summed, T)
            pool.wait_ge(lists_ready, 1)

            def gather(s, t):
                if not (isinstance(t, int) and t < 2):
                    pool.wait_ge(b_made, t - 1)
                nc.gpsimd.tensor_copy(list_now[s][:, :, :].rearrange("p a q -> p (a q)"),
                                      lists[:, bass.ds(t, 1), :, :].rearrange("p o a q -> p (o a q)")).then_inc(list_taken, 1)
                pool.wait_ge(zero_stored, 16)
                pool.wait_ge(list_taken, t + 1)
                pool.nop(nofuse=True)
                for q in range(LISTS):
                    pool.indirect_dma_start(out=edge[s][:, q, :], out_offset=None, in_=at_dram,
                                            in_offset=bass.IndirectOffsetOnAxis(ap=list_now[s][:, 1, q:q + 1], axis=0)).then_inc(edges_in[s], 16)
                for q in range(LISTS):
                    pool.indirect_dma_start(out=edge_w[s][:, q:q + 1], out_offset=None, in_=w_dram,
                                            in_offset=bass.IndirectOffsetOnAxis(ap=list_now[s][:, 0, q:q + 1], axis=0)).then_inc(edge_w_in[s], 16)
                for q in range(LISTS):
                    pool.indirect_dma_start(out=rows[s][q][:, :], out_offset=None, in_=adj,
                                            in_offset=bass.IndirectOffsetOnAxis(ap=list_now[s][:, 0, q:q + 1], axis=0)).then_inc(rows_in[s][q], 16)
                pool.wait_ge(own_scaled, t + 1)
                nc.gpsimd.tensor_tensor(own[s][:, :], own_raw[s][:, :], t0_ident[:, :], ALU.add).then_inc(own_ready, 1)

            def pick(r, t):
                if not (isinstance(t, int) and t < PICKS):
                    pool.wait_ge(hs_ready, t - PICKS + 1)
                pool.wait_ge(xw_stored, 16)
                pool.wait_ge(idx_ready, t + 1)
                pool.nop(nofuse=True)
                for m in range(TOPK):
                    pool.indirect_dma_start(out=picked[r][:, m, :], out_offset=None, in_=xw_dram,
                                            in_offset=bass.IndirectOffsetOnAxis(ap=idx[r][:, m:m + 1], axis=0)).then_inc(picks_in[r], 16)

            def weigh_all(s, n, t):
                pool.wait_ge(all_in[s], 16 * n + 16)
                nc.gpsimd.tensor_tensor(all_edges[s], all_edges[s], w[:, :, None].to_broadcast([P, T, P]), ALU.mult).then_inc(all_scaled, 1)
                pool.wait_ge(all_scaled, t + 1)
                nc.gpsimd.tensor_tensor(tile_of(all_edges[s], t), tile_of(all_edges[s], t), t0_ident[:, :], ALU.add).then_inc(all_ready, 1)

            overflow = overflow_flag(pool)
            with pool.If(overflow == 0):
                for t in range(AHEAD):
                    gather(t % 2, t)
                for t in range(PICKS):
                    gather(t % 2, t + AHEAD)
                    pick(t, t)
                with pool.Fori(1, T // PICKS - 1) as i:
                    for j in range(PICKS):
                        gather(j % 2, PICKS * i + j + AHEAD)
                        pick(j, PICKS * i + j)
                for t in range(T - AHEAD, T):
                    pick(t % PICKS, t)
            with pool.Else():
                for t in range(PICKS + 2):
                    weigh_all(t % 2, t // 2, t)
                    if t >= 2:
                        pick(t - 2, t - 2)
                with pool.Fori(1, T // PICKS - 1) as i:
                    for j in range(PICKS):
                        weigh_all(j % 2, 2 * i + j // 2 + 1, PICKS * i + j + 2)
                        pick(j, PICKS * i + j)
                for t in range(T - PICKS, T):
                    if t + 2 < T:
                        weigh_all(t % 2, t // 2 + 1, t + 2)
                    pick(t % PICKS, t)


_INS = ["x", "adj", "L0_gnn_theta", "L0_gnn_W", "L0_gnn_b"]


def kernel(**inputs):
    import numpy as _np
    import concourse.bacc as _bacc
    from concourse import mybir as _mybir
    from concourse.bass_utils import run_bass_kernel_spmd as _run

    nc = _bacc.Bacc("TRN2", target_bir_lowering=False, num_devices=1)
    arrays, args = {}, []
    for name in _INS:
        a = _np.ascontiguousarray(inputs[name])
        arrays[f"in_{name}_dram"] = a
        args.append(nc.dram_tensor(f"in_{name}_dram", a.shape, _mybir.dt.from_np(a.dtype), kind="ExternalInput").ap())
    out = nc.dram_tensor("out_0_dram", inputs["x"].shape, _mybir.dt.float32, kind="ExternalOutput").ap()
    adjacency_resnorm(nc, *args, out)
    r = _run(nc, [arrays], core_ids=[0])
    return r.results[0]["out_0_dram"]
```

```python
import concourse.bass as bass
from concourse import mybir
from contextlib import ExitStack


def adjacency_resnorm(nc, x, adj, theta, W, b, out):
    fp32 = mybir.dt.float32
    fp16 = mybir.dt.float16
    bf16 = mybir.dt.bfloat16
    u32 = mybir.dt.uint32
    ALU = mybir.AluOpType
    ACT = mybir.ActivationFunctionType
    AX = mybir.AxisListType

    P = 128
    N = adj.shape[0]
    D = x.shape[1]
    T = N // P
    BANK = 512
    NB = N // BANK
    TOPK = 4
    EPS = 1e-5
    LISTS = 2
    SLOTS = LISTS * P
    HALF = T // 2
    LOOK = 3
    STAGES = 4
    PICKS = 4
    AHEAD = 4
    LOOKED_AT = 384
    SUMS_AT = 3 * BANK
    EARLY = 2

    with ExitStack() as ctx:
        def sb(name, shape, dt=fp32):
            return ctx.enter_context(nc.sbuf_tensor(name, shape, dt))

        def sem(name):
            return ctx.enter_context(nc.semaphore(name))

        at_dram = nc.dram_tensor("at_dram", [T * N + 1, P + 1], fp32, kind="Internal").ap()
        at_tiles = at_dram[1:, :].rearrange("(t p j) i -> t p j i", t=T, j=T)
        xw_dram = nc.dram_tensor("xw_dram", [N, D], fp32, kind="Internal").ap()
        vec_dram = [nc.dram_tensor(f"vec_dram{n}", [P, T], fp32, kind="Internal").ap() for n in range(3)]

        A = sb("A", [P, T, N])
        big = [sb(f"big{n}", [P, N]) for n in range(STAGES)]
        stage = big
        rows = [big[0:2], big[2:4]]
        at = [sb(f"at{s}", [P, T, P + 1]) for s in range(2)]
        G = [at[s][:, :, :].rearrange("p j i -> p (j i)")[:, 0:N] for s in range(2)]
        all_edges = [big[2 * s][:, :].rearrange("p (j i) -> p j i", j=T) for s in range(2)]
        vec = sb("vec", [P, N])
        junk = sb("junk", [P, N], bf16)
        ident = sb("ident", [P, P])
        t0_ident = sb("t0_ident", [P, P])
        ones = sb("ones", [P, P])
        ones_b = sb("ones_b", [P, 1], bf16)
        my_slot = sb("my_slot", [P, 2 * T])
        tile_base = sb("tile_base", [P, 2 * T])
        tile_row = sb("tile_row", [P, 2 * T])
        part_no = sb("part_no", [P, 1])
        par4 = sb("par4", [P, 2, 4])
        parity = sb("parity", [P, 2])
        count = sb("count", [P, 2])
        prefix = sb("prefix", [P, 2, P + LOOK], fp16)
        start = sb("start", [P, 2])
        end = sb("end", [P, 2])
        over = sb("over", [P, 2])
        over_sum = sb("over_sum", [P, 1])
        flag = sb("flag", [P, 1], u32)
        looked = sb("looked", [P, 2 * T, LOOK])
        local = sb("local", [P, 2 * T])
        signs = sb("signs", [P, 2 * T])
        node = sb("node", [P, 2 * T])
        node_at = sb("node_at", [P, 2 * T])
        lists = sb("lists", [P, T, 2, LISTS], u32)
        list_now = [sb(f"list_now{s}", [P, 2, LISTS], u32) for s in range(2)]
        t01 = sb("t01", [P, 2])
        d = sb("d", [P, T])
        root = sb("root", [P, T])
        y = sb("y", [P, T])
        tmp = sb("tmp", [P, T])
        tmp2 = sb("tmp2", [P, T])
        y2 = sb("y2", [P, T])
        w = sb("w", [P, T])
        r1 = sb("r1", [P, T])
        v = sb("v", [P, T])
        r2 = sb("r2", [P, T])
        d2 = sb("d2", [P, T])
        c = sb("c", [P, T])
        dc = sb("dc", [P, T])
        hs = sb("hs", [P, T, D])
        Ws = sb("Ws", [D, D])
        WT = sb("WT", [D, D])
        b_all = sb("b_all", [P, D])
        edge = [sb(f"edge{s}", [P, LISTS, P + 1]) for s in range(2)]
        own_raw = [sb(f"own_raw{s}", [P, P]) for s in range(2)]
        own = [sb(f"own{s}", [P, P]) for s in range(2)]
        top = [sb(f"top{s}", [P, 8]) for s in range(PICKS)]
        idx = [sb(f"idx{s}", [P, 8], u32) for s in range(PICKS)]
        coef = [sb(f"coef{s}", [P, 8]) for s in range(PICKS)]
        picked = [sb(f"picked{s}", [P, TOPK, D]) for s in range(PICKS)]
        mean = sb("mean", [P, T])
        var = sb("var", [P, T])
        std = sb("std", [P, T])
        rstd = sb("rstd", [P, T])
        xT = G[1][0:D, :].rearrange("f (t p) -> f t p", t=T)
        xw = vec[:, 0:T * D].rearrange("p (t f) -> p t f", t=T)
        not_own = picked[0][:, :, :].rearrange("p m f -> p (m f)").rearrange("p (t j) -> p t j", t=T)
        before = picked[1][:, 0:2, :].rearrange("p m f -> p (m f)")
        slot_no = picked[2][:, :, :].rearrange("p m f -> p (m f)")
        zero_row = picked[3][:, :, :].rearrange("p m f -> p (m f)")[0:1, 0:P + 1]
        mask = big[0][:, 0:T * T].rearrange("p (t j) -> p t j", t=T)
        past = big[0][:, BANK:BANK + 2 * SLOTS].rearrange("p (h s) -> p h s", h=2)
        inside = big[0][:, 2 * BANK:2 * BANK + 2 * SLOTS].rearrange("p (h s) -> p h s", h=2)
        pick_block = big[1][:, 0:2 * SLOTS].bitcast(fp16).rearrange("p (h r s) -> p h r s", h=2, r=2)
        sq = big[0][:, 0:T * D].rearrange("p (t f) -> p t f", t=T)

        ps = [ctx.enter_context(nc.psum_tensor(f"ps{s}", [P, N], fp32)) for s in range(2)]

        small_in = sem("small_in")
        consts = sem("consts")
        making = sem("making")
        t01_ready = sem("t01_ready")
        d2_ready = sem("d2_ready")
        x_turned = sem("x_turned")
        x_turned_out = sem("x_turned_out")
        xw_made = sem("xw_made")
        xw_out = sem("xw_out")
        xw_stored = sem("xw_stored")
        zero_stored = sem("zero_stored")
        loaded = [sem(f"loaded{s}") for s in range(STAGES)]
        resident = sem("resident")
        turned = sem("turned")
        turned_out = sem("turned_out")
        col_summed = sem("col_summed")
        w_placed = sem("w_placed")
        at_stored = [sem(f"at_stored{s}") for s in range(2)]
        rooted = sem("rooted")
        step = sem("step")
        col_ready = sem("col_ready")
        w_ready = sem("w_ready")
        vec_stored = [sem(f"vec_stored{n}") for n in range(3)]
        vec_spread = [sem(f"vec_spread{n}") for n in range(3)]
        mask_ready = sem("mask_ready")
        mask_turned = sem("mask_turned")
        prefix_ready = sem("prefix_ready")
        start_made = sem("start_made")
        over_ready = sem("over_ready")
        over_made = sem("over_made")
        flag_ready = sem("flag_ready")
        blocks_ready = sem("blocks_ready")
        looked_made = sem("looked_made")
        prefix_made = sem("prefix_made")
        local_ready = sem("local_ready")
        counted = sem("counted")
        listing = sem("listing")
        lists_ready = sem("lists_ready")
        list_taken = sem("list_taken")
        edges_in = [sem(f"edges_in{s}") for s in range(2)]
        rows_in = [[sem(f"rows_in{s}{q}") for q in range(LISTS)] for s in range(2)]
        own_in = [sem(f"own_in{s}") for s in range(2)]
        edges_ready = sem("edges_ready")
        all_in = [sem(f"all_in{s}") for s in range(2)]
        all_scaled = sem("all_scaled")
        all_ready = sem("all_ready")
        own_scaled = sem("own_scaled")
        own_ready = sem("own_ready")
        b_made = sem("b_made")
        b_out = sem("b_out")
        pass1 = sem("pass1")
        pass2 = sem("pass2")
        g_scaled = sem("g_scaled")
        g_ready = sem("g_ready")
        top_ready = sem("top_ready")
        idx_ready = sem("idx_ready")
        coef_ready = sem("coef_ready")
        picks_in = [sem(f"picks_in{s}") for s in range(PICKS)]
        weighted = sem("weighted")
        pairs = sem("pairs")
        summed = sem("summed")
        hs_ready = sem("hs_ready")
        ln_var = sem("ln_var")
        ln_root = sem("ln_root")
        finished = sem("finished")
        out_stored = sem("out_stored")

        def tile_of(buffer3, t):
            return buffer3[:, bass.ds(t, 1), :].rearrange("p o f -> p (o f)")

        def overflow_flag(engine):
            engine.wait_ge(flag_ready, 1)
            return engine.value_load(flag[0:1, 0:1])

        block = ctx.enter_context(nc.Block())

        @block.sync
        def _(sp):
            adj_tiles = adj.rearrange("(p t) k -> t p k", t=T)
            for s in range(STAGES):
                sp.dma_start(stage[s][:, :], adj_tiles[s]).then_inc(loaded[s], 16)
            with sp.Fori(1, T // STAGES) as i:
                for s in range(STAGES):
                    sp.wait_ge(resident, STAGES * (i - 1) + s + 1)
                    sp.wait_ge(col_summed, STAGES * (i - 1) + s + 1)
                    sp.dma_start(stage[s][:, :], adj_tiles[bass.ds(STAGES * i + s, 1)].rearrange("o p k -> p (o k)")).then_inc(loaded[s], 16)
            sp.wait_ge(col_ready, 1)
            sp.wait_ge(xw_stored, 16)
            sp.dma_start(vec_dram[0], y[:, :]).then_inc(vec_stored[0], 16)
            sp.wait_ge(vec_stored[0], 16)
            sp.dma_start(vec[:, :], vec_dram[0].rearrange("p t -> (p t)").rearrange("(o k) -> o k", o=1).to_broadcast([P, N])).then_inc(vec_spread[0], 16)
            def spread(n, vector):
                sp.wait_ge(col_ready, n + 1)
                sp.dma_start(vec_dram[n], vector[:, :]).then_inc(vec_stored[n], 16)
                sp.wait_ge(vec_stored[n], 16)
                sp.dma_start(vec[:, :], vec_dram[n].rearrange("p t -> (p t)").rearrange("(o k) -> o k", o=1).to_broadcast([P, N])).then_inc(vec_spread[n], 16)

            def own_rows(s, t):
                sp.dma_start(own_raw[s][:, :], at_tiles[bass.ds(t, 1), :, bass.ds(t, 1), 0:P].rearrange("a p b i -> p (a b i)")).then_inc(own_in[s], 16)

            def all_rows(s, t):
                sp.dma_start(all_edges[s], at_tiles[bass.ds(t, 1), :, :, 0:P].rearrange("o p j i -> p (o j) i")).then_inc(all_in[s], 16)

            overflow = overflow_flag(sp)
            with sp.If(overflow == 0):
                for s in range(2):
                    sp.wait_ge(at_stored[s], 16)
                    own_rows(s, s)
                for s in range(2):
                    sp.wait_ge(own_ready, s + 1)
                    sp.wait_ge(at_stored[s], 16 * 2)
                    own_rows(s, s + 2)
                    if s == 0:
                        spread(1, v)
                spread(2, c)
                for s in range(2):
                    sp.wait_ge(at_stored[s], 16 * HALF)
                with sp.Fori(2, T // 2) as i:
                    for s in range(2):
                        sp.wait_ge(own_ready, 2 * i + s - 1)
                        own_rows(s, 2 * i + s)
            with sp.Else():
                sp.wait_ge(lists_ready, 1)
                sp.wait_ge(counted, 2 * T)
                sp.wait_ge(resident, T)
                sp.wait_ge(col_summed, T)
                for s in range(2):
                    sp.wait_ge(at_stored[s], 16 * HALF)
                    all_rows(s, s)
                spread(1, v)
                spread(2, c)
                with sp.Fori(1, T // 2) as i:
                    for s in range(2):
                        sp.wait_ge(b_made, 2 * i + s - 1)
                        all_rows(s, 2 * i + s)
            sp.wait_ge(finished, 1)
            sp.dma_start(out.rearrange("(p t) f -> p t f", t=T), hs[:, :, :]).then_inc(out_stored, 16)
            sp.wait_ge(out_stored, 16)

        @block.scalar
        def _(act):
            act.dma_start(hs[:, :, :], x.rearrange("(p t) f -> p t f", t=T)).then_inc(small_in, 16)
            act.dma_start(Ws[:, :], W).then_inc(small_in, 16)
            act.dma_start(t01[:, :], theta.rearrange("(o k) -> o k", o=1).to_broadcast([P, 2])).then_inc(small_in, 16)
            act.dma_start(b_all[:, :], b.rearrange("(o k) -> o k", o=1).to_broadcast([P, D])).then_inc(small_in, 16)
            act.wait_ge(small_in, 64)
            nc.scalar.activation(t01[:, :], t01[:, :], ACT.Sigmoid).then_inc(t01_ready, 1)
            with act.Fori(0, T // STAGES) as i:
                for s in range(STAGES):
                    act.wait_ge(loaded[s], 16 * i + 16)
                    nc.scalar.activation(tile_of(A, STAGES * i + s), stage[s][:, :], ACT.Copy,
                                         accum_out=d[:, bass.ds(STAGES * i + s, 1)]).then_inc(resident, 1)
            act.wait_ge(resident, T)
            nc.scalar.activation(root[:, :], d[:, :], ACT.Sqrt).then_inc(rooted, 1)

            def take_turned(t):
                s = t % 2
                room = ps[0] if t < EARLY else ps[1]
                for h in range(2):
                    act.wait_ge(turned, 2 * t + h + 1)
                    if h == 0 and t >= 2:
                        act.wait_ge(at_stored[s], 16 * (t // 2))
                    nc.scalar.activation(at[s][:, h * HALF:(h + 1) * HALF, 0:P],
                                         room[:, h * 2 * BANK:(h + 1) * 2 * BANK].rearrange("p (j i) -> p j i", j=HALF),
                                         ACT.Copy).then_inc(turned_out, 1)
                if t < 2:
                    act.wait_ge(w_ready, 1)
                    nc.scalar.activation(at[s][:, :, P], w[:, :], ACT.Copy).then_inc(w_placed, 1)
                    act.wait_ge(w_placed, t + 1)
                act.wait_ge(turned_out, 2 * t + 2)
                act.dma_start(at_tiles[t], at[s][:, :, :]).then_inc(at_stored[s], 16)

            for t in range(EARLY):
                take_turned(t)
            act.wait_ge(local_ready, 1)
            for h in range(2):
                act.wait_ge(prefix_made, h + 1)
                for n in range(T):
                    nc.scalar.activation(junk[:, n * P:(n + 1) * P], ps[0][:, n * P:(n + 1) * P], ACT.Sign, scale=-1.0,
                                         bias=local[:, n + h * T:n + h * T + 1],
                                         accum_out=signs[:, n + h * T:n + h * T + 1]).then_inc(counted, 1)
                if h == 0:
                    take_turned(2)
                    act.wait_ge(counted, T)
            take_turned(3)

            def edges(s, n, t):
                act.wait_ge(own_in[s], 16 * n + 16)
                nc.scalar.activation(own_raw[s][:, :], own_raw[s][:, :], ACT.Copy,
                                     scale=w[:, bass.ds(t, 1)]).then_inc(own_scaled, 1)
                act.wait_ge(edges_in[s], 32 * n + 32)
                for q in range(LISTS):
                    last = nc.scalar.activation(edge[s][:, q, 0:P], edge[s][:, q, 0:P], ACT.Copy, scale=edge[s][:, q, P:P + 1])
                last.then_inc(edges_ready, 1)

            def take_b(s, t):
                act.wait_ge(b_made, t + 1)
                if isinstance(t, int) and t < 2:
                    act.wait_ge(at_stored[s], 16 * HALF)
                else:
                    act.wait_ge(idx_ready, t - 1)
                nc.scalar.activation(G[s], ps[s][:, :], ACT.Copy).then_inc(b_out, 1)

            def root_d2():
                act.wait_ge(d2_ready, 1)
                nc.scalar.activation(root[:, :], d2[:, :], ACT.Sqrt).then_inc(rooted, 1)

            overflow = overflow_flag(act)
            with act.If(overflow == 0):
                for t in range(4, T):
                    take_turned(t)
                    if t == 6:
                        edges(0, 0, 0)
                    if t == 10:
                        edges(1, 0, 1)
                take_b(0, 0)
                edges(0, 1, 2)
                take_b(1, 1)
                edges(1, 1, 3)
                root_d2()
                with act.Fori(1, T // 2 - 1) as i:
                    for s in range(2):
                        take_b(s, 2 * i + s)
                        edges(s, i + 1, 2 * i + s + 2)
                take_b(0, T - 2)
                take_b(1, T - 1)
            with act.Else():
                for t in range(4, T):
                    take_turned(t)
                take_b(0, 0)
                take_b(1, 1)
                root_d2()
                with act.Fori(1, T // 2) as i:
                    for s in range(2):
                        take_b(s, 2 * i + s)
            act.wait_ge(ln_var, 1)
            nc.scalar.activation(std[:, :], var[:, :], ACT.Sqrt).then_inc(ln_root, 1)

        @block.tensor
        def _(pe):
            pe.wait_ge(consts, 1)
            pe.wait_ge(small_in, 64)
            for t in range(T):
                nc.tensor.transpose(ps[0][0:D, t * P:(t + 1) * P], hs[:, t, :], ident[:, :])
            nc.tensor.transpose(ps[1][0:D, 0:D], Ws[:, :], ident[0:D, 0:D]).then_inc(x_turned, 1)

            def column_sums(s, i):
                upper = stage[s][:, :].bitcast(bf16)[:, 1:2 * N:2]
                pe.wait_ge(loaded[s], 16 * i + 16)
                for j in range(T):
                    mm = nc.tensor.matmul(ps[1][:, bass.ds(SUMS_AT + (STAGES * i + s) * T + j, 1)], upper[:, j:N:T], ones_b[:, :],
                                          start=True, stop=True, skip_group_check=True)
                mm.then_inc(col_summed, 1)

            column_sums(0, 0)
            column_sums(1, 0)
            pe.wait_ge(x_turned_out, 1)
            for t in range(T):
                mm = nc.tensor.matmul(ps[1][:, t * D:(t + 1) * D], xT[:, t, :], WT[:, :], start=True, stop=True)
            mm.then_inc(xw_made, 1)
            column_sums(2, 0)
            column_sums(3, 0)
            with pe.Fori(1, T // STAGES) as i:
                for s in range(STAGES):
                    column_sums(s, i)

            def turn(t):
                pe.wait_ge(resident, T)
                room = ps[0] if t < EARLY else ps[1]
                for h in range(2):
                    if t not in (0, EARLY):
                        pe.wait_ge(turned_out, 2 * t + h - 1)
                    for j in range(h * HALF, (h + 1) * HALF):
                        mm = nc.tensor.transpose(room[:, j * P:(j + 1) * P], A[:, t, j:N:T], ident[:, :])
                    mm.then_inc(turned, 1)

            pe.wait_ge(xw_out, 1)
            pe.wait_ge(mask_ready, 1)
            for h in range(2):
                mm = nc.tensor.transpose(ps[1][:, BANK + h * P:BANK + (h + 1) * P],
                                         mask[:, h * HALF:(h + 1) * HALF, :].rearrange("p t j -> p (t j)"), ident[:, :])
            mm.then_inc(mask_turned, 1)
            turn(0)
            pe.wait_ge(prefix_ready, 1)
            nc.tensor.matmul(ps[1][:, 2 * BANK:2 * BANK + 2], before, count[:, :], start=True, stop=True).then_inc(start_made, 1)
            turn(1)
            pe.wait_ge(over_ready, 1)
            nc.tensor.matmul(ps[1][:, 2 * BANK + 8:2 * BANK + 10], ones[:, :], over[:, :], start=True, stop=True).then_inc(over_made, 1)
            pe.wait_ge(blocks_ready, 1)
            pe.wait_ge(flag_ready, 1)
            for t in range(T):
                h, g, r = t // HALF, (t % HALF) // 2, t % 2
                k = slice(32 * g, 32 * g + 32)
                for q in range(LISTS):
                    at = g * BANK + LOOKED_AT + ((h * 2 + r) * LISTS + q) * LOOK
                    mm = nc.tensor.matmul(ps[1][:, at:at + LOOK], pick_block[k, h, r, q * P:(q + 1) * P],
                                          prefix[k, h, P:P + LOOK], start=True, stop=True, skip_group_check=True)
            mm.then_inc(looked_made, 1)
            for h in range(2):
                if h == 1:
                    pe.wait_ge(counted, T)
                else:
                    pe.wait_ge(turned_out, 2 * EARLY)
                for t in range(HALF):
                    g, r = t // 2, t % 2
                    k = slice(32 * g, 32 * g + 32)
                    for q in range(LISTS):
                        at = (t * LISTS + q) * P
                        mm = nc.tensor.matmul(ps[0][:, at:at + P], pick_block[k, h, r, q * P:(q + 1) * P],
                                              prefix[k, h, 0:P], start=True, stop=True, skip_group_check=True)
                mm.then_inc(prefix_made, 1)
                if h == 0:
                    pe.wait_ge(local_ready, 1)
                    turn(2)
            turn(3)

            def product(s, n, t, between=()):
                pe.wait_ge(own_ready, t + 1)
                pe.wait_ge(edges_ready, t + 1)
                if isinstance(t, int) and t == 0:
                    pe.wait_ge(counted, 2 * T)
                elif isinstance(t, int) and t == 1:
                    pe.wait_ge(turned_out, 2 * T)
                else:
                    pe.wait_ge(b_out, t - 1)
                for k in range(LISTS + 1):
                    if k:
                        for other in between[k - 1:k]:
                            turn(other)
                        pe.wait_ge(rows_in[s][k - 1], 16 * n + 16)
                    for m in range(NB):
                        cols = slice(m * BANK, (m + 1) * BANK)
                        if k:
                            mm = nc.tensor.matmul(ps[s][:, cols], edge[s][:, k - 1, 0:P], rows[s][k - 1][:, cols],
                                                  start=False, stop=(k == LISTS), skip_group_check=True)
                        else:
                            mm = nc.tensor.matmul(ps[s][:, cols], own[s][:, :],
                                                  A[:, bass.ds(t, 1), cols].rearrange("p o k -> p (o k)"),
                                                  start=True, stop=False, skip_group_check=True)
                mm.then_inc(b_made, 1)

            def product_of_all(s, t):
                pe.wait_ge(all_ready, t + 1)
                if isinstance(t, int) and t == 0:
                    pe.wait_ge(counted, 2 * T)
                elif isinstance(t, int) and t == 1:
                    pe.wait_ge(turned_out, 2 * T)
                else:
                    pe.wait_ge(b_out, t - 1)
                for j in range(T):
                    for m in range(NB):
                        cols = slice(m * BANK, (m + 1) * BANK)
                        mm = nc.tensor.matmul(ps[s][:, cols], all_edges[s][:, j, :], A[:, j, cols],
                                              start=(j == 0), stop=(j == T - 1), skip_group_check=True)
                mm.then_inc(b_made, 1)

            overflow = overflow_flag(pe)
            with pe.If(overflow == 0):
                for t in range(4, 8):
                    turn(t)
                product(0, 0, 0, between=(8, 9))
                for t in range(10, T):
                    turn(t)
                product(1, 0, 1)
                with pe.Fori(1, T // 2) as i:
                    for s in range(2):
                        product(s, i, 2 * i + s)
            with pe.Else():
                for t in range(4, T):
                    turn(t)
                product_of_all(0, 0)
                product_of_all(1, 1)
                with pe.Fori(1, T // 2) as i:
                    for s in range(2):
                        product_of_all(s, 2 * i + s)

        @block.vector
        def _(dve):
            chain = [0]

            def done(ins):
                chain[0] += 1
                ins.then_inc(step, 1)
                dve.wait_ge(step, chain[0])

            dve.wait_ge(x_turned, 1)
            nc.vector.tensor_copy(xT[:, :, :], ps[0][0:D, :].rearrange("f (t p) -> f t p", t=T))
            nc.vector.tensor_copy(WT[:, :], ps[1][0:D, 0:D]).then_inc(x_turned_out, 1)
            nc.vector.tensor_tensor(hs[:, :, :], hs[:, :, :], b_all[:, None, :].to_broadcast([P, T, D]), ALU.add)
            dve.wait_ge(xw_made, 1)
            nc.vector.tensor_copy(xw, ps[1][:, 0:T * D].rearrange("p (t f) -> p t f", t=T)).then_inc(xw_out, 1)

            def inverse_root(dst, src):
                done(nc.vector.reciprocal(tmp[:, :], root[:, :]))
                done(nc.vector.tensor_tensor(tmp2[:, :], tmp[:, :], tmp[:, :], ALU.mult))
                done(nc.vector.tensor_tensor(tmp2[:, :], tmp2[:, :], src[:, :], ALU.mult))
                done(nc.vector.tensor_scalar(tmp2[:, :], tmp2[:, :], -0.5, 1.5, ALU.mult, ALU.add))
                done(nc.vector.tensor_tensor(dst[:, :], tmp[:, :], tmp2[:, :], ALU.mult))

            dve.wait_ge(col_summed, T)
            dve.wait_ge(consts, 2)
            dve.wait_ge(resident, T)
            nc.vector.scalar_tensor_tensor(out=mask, in0=ps[1][:, SUMS_AT:SUMS_AT + T * T].rearrange("p (t j) -> p t j", t=T), scalar=0.0,
                                           in1=not_own, op0=ALU.not_equal, op1=ALU.mult).then_inc(mask_ready, 1)
            dve.wait_ge(rooted, 1)
            inverse_root(y, d)
            nc.vector.tensor_tensor(y2[:, :], y[:, :], y[:, :], ALU.mult).then_inc(col_ready, 1)
            dve.wait_ge(mask_turned, 1)
            for h in range(2):
                done(nc.vector.tensor_tensor_scan(out=prefix[:, h, 0:P], data0=ones[:, :], data1=ps[1][:, BANK + h * P:BANK + (h + 1) * P],
                                                  initial=0.0, op0=ALU.mult, op1=ALU.add))
            nc.vector.tensor_copy(count[:, :], prefix[:, :, P - 1]).then_inc(prefix_ready, 1)
            dve.wait_ge(t01_ready, 1)
            nc.vector.tensor_scalar(w[:, :], y2[:, :], t01[:, 1:2], None, ALU.mult).then_inc(w_ready, 1)
            dve.wait_ge(start_made, 1)
            done(nc.vector.tensor_copy(start[:, :], ps[1][:, 2 * BANK:2 * BANK + 2]))
            done(nc.vector.tensor_tensor(end[:, :], start[:, :], count[:, :], ALU.add))
            nc.vector.tensor_scalar(over[:, :], end[:, :], float(SLOTS), None, ALU.is_gt).then_inc(over_ready, 1)
            for h in range(2):
                nc.vector.tensor_copy(prefix[:, h, P:P + 1], start[:, h:h + 1])
                nc.vector.tensor_copy(prefix[:, h, P + 1:P + 2], part_no[:, :])
                nc.vector.memset(prefix[:, h, P + 2:P + 3], 1.0)
                done(nc.vector.tensor_scalar(past[:, h, :], slot_no, end[:, h:h + 1], None, ALU.is_ge))
                done(nc.vector.scalar_tensor_tensor(out=inside[:, h, :], in0=slot_no, scalar=start[:, h:h + 1],
                                                    in1=past[:, h, :], op0=ALU.is_ge, op1=ALU.subtract))
                for r in range(2):
                    last = nc.vector.tensor_scalar(pick_block[:, h, r, :], inside[:, h, :], parity[:, r:r + 1], None, ALU.mult)
            last.then_inc(blocks_ready, 1)
            dve.wait_ge(over_made, 1)
            done(nc.vector.tensor_reduce(over_sum[:, :], ps[1][:, 2 * BANK + 8:2 * BANK + 10], AX.X, ALU.add))
            nc.vector.tensor_copy(flag[:, :], over_sum[:, :]).then_inc(flag_ready, 1)
            dve.wait_ge(looked_made, 1)
            banks = ps[1][:, :].rearrange("p (g n) -> p g n", g=NB)[:, :, LOOKED_AT:LOOKED_AT + 4 * LISTS * LOOK]
            looked_v = looked[:, :, :].rearrange("p (h g rq) l -> p h g rq l", h=2, g=NB)
            for h in range(2):
                last = nc.vector.tensor_copy(looked_v[:, h], banks.rearrange("p g (h rq l) -> p h g rq l", h=2, l=LOOK)[:, h])
            done(last)
            done(nc.vector.tensor_tensor(local[:, :], my_slot[:, :], looked[:, :, 0], ALU.subtract))
            nc.vector.tensor_scalar(local[:, :], local[:, :], 0.5, None, ALU.add).then_inc(local_ready, 1)
            for n, (result, passed) in enumerate(((r1, pass1), (r2, pass2))):
                dve.wait_ge(vec_spread[n], 16)
                if n == 0:
                    dve.wait_ge(counted, 2 * T)
                with dve.Fori(0, T // 8) as i:
                    for j in range(8):
                        nc.vector.scalar_tensor_tensor(out=junk[:, :], in0=tile_of(A, 8 * i + j), scalar=1.0, in1=vec[:, :],
                                                       op0=ALU.mult, op1=ALU.mult, accum_out=result[:, bass.ds(8 * i + j, 1)]).then_inc(passed, 1)
                        dve.wait_ge(passed, 8 * i + j + 1)
                if n == 0:
                    dve.wait_ge(pass1, T)
                    done(nc.vector.tensor_tensor(v[:, :], y2[:, :], r1[:, :], ALU.mult))
                    nc.vector.tensor_scalar(tmp[:, :], r1[:, :], t01[:, 0:1], None, ALU.mult).then_inc(col_ready, 1)
            dve.wait_ge(col_ready, 2)
            done(nc.vector.scalar_tensor_tensor(out=tmp2[:, :], in0=r2[:, :], scalar=t01[:, 1:2], in1=tmp[:, :], op0=ALU.mult, op1=ALU.add))
            done(nc.vector.tensor_tensor(tmp[:, :], tmp2[:, :], y[:, :], ALU.mult))
            done(nc.vector.tensor_scalar(d2[:, :], tmp[:, :], 1.0, None, ALU.add))
            nc.vector.tensor_copy(tmp[:, :], d2[:, :]).then_inc(d2_ready, 1)
            dve.wait_ge(rooted, 2)
            dve.wait_ge(d2_ready, 1)
            inverse_root(c, d2)
            done(nc.vector.tensor_tensor(c[:, :], c[:, :], y[:, :], ALU.mult))
            nc.vector.tensor_tensor(dc[:, :], c[:, :], d[:, :], ALU.mult).then_inc(col_ready, 1)
            dve.wait_ge(vec_spread[2], 16)
            dve.wait_ge(col_ready, 3)

            def scale(s, t):
                dve.wait_ge(b_out, t + 1)
                nc.vector.tensor_tensor(G[s], G[s], vec[:, :], ALU.mult).then_inc(g_scaled, 1)
                dve.wait_ge(g_scaled, t + 1)
                diagonal = G[s].rearrange("p (k o) -> p k o", o=T)[:, :, bass.ds(t, 1)].rearrange("p k o -> p (k o)")
                nc.vector.scalar_tensor_tensor(out=diagonal, in0=ident[:, :], scalar=dc[:, bass.ds(t, 1)], in1=diagonal,
                                               op0=ALU.mult, op1=ALU.add).then_inc(g_ready, 1)

            def find(s, r, t):
                nc.vector.max(out=top[r][:, :], in_=G[s]).then_inc(top_ready, 1)
                dve.wait_ge(top_ready, t + 1)
                nc.vector.tensor_scalar(coef[r][:, :], top[r][:, :], c[:, bass.ds(t, 1)], None, ALU.mult).then_inc(coef_ready, 1)
                nc.vector.max_index(out=idx[r][:, :], in_max=top[r][:, :], in_values=G[s]).then_inc(idx_ready, 1)

            def add_picked(r, n, t, g_tile=None):
                dve.wait_ge(picks_in[r], 16 * TOPK * (n + 1))
                dve.wait_ge(coef_ready, t + 1)
                if g_tile is not None:
                    dve.wait_ge(g_ready, g_tile + 1)
                nc.vector.tensor_tensor(picked[r][:, :, :], picked[r][:, :, :], coef[r][:, 0:TOPK, None].to_broadcast([P, TOPK, D]),
                                        ALU.mult).then_inc(weighted, 1)
                dve.wait_ge(weighted, t + 1)
                nc.vector.tensor_tensor(picked[r][:, 0:2, :], picked[r][:, 0:2, :], picked[r][:, 2:4, :], ALU.add).then_inc(pairs, 1)
                dve.wait_ge(pairs, t + 1)
                nc.vector.tensor_tensor(picked[r][:, 0, :], picked[r][:, 0, :], picked[r][:, 1, :], ALU.add).then_inc(summed, 1)
                dve.wait_ge(summed, t + 1)
                nc.vector.tensor_tensor(tile_of(hs, t), tile_of(hs, t), picked[r][:, 0, :], ALU.add).then_inc(hs_ready, 1)

            for t in range(2):
                scale(t, t)
                dve.wait_ge(g_ready, t + 1)
                find(t, t, t)
            with dve.Fori(0, (T - 4) // PICKS) as i:
                for j in range(PICKS):
                    scale(j % 2, 4 * i + j + 2)
                    add_picked(j, i, 4 * i + j, 4 * i + j + 2)
                    find(j % 2, (j + 2) % PICKS, 4 * i + j + 2)
            for t in range(T - 2, T):
                scale(t % 2, t)
                add_picked((t - 2) % PICKS, (t - 2) // PICKS, t - 2, t)
                find(t % 2, t % PICKS, t)
            for t in range(T - 2, T):
                add_picked(t % PICKS, t // PICKS, t)
            dve.wait_ge(hs_ready, T)
            done(nc.vector.tensor_reduce(mean[:, :], hs[:, :, :], AX.X, ALU.add))
            done(nc.vector.tensor_scalar(mean[:, :], mean[:, :], 1.0 / D, None, ALU.mult))
            done(nc.vector.tensor_tensor(hs[:, :, :], hs[:, :, :], mean[:, :, None].to_broadcast([P, T, D]), ALU.subtract))
            done(nc.vector.tensor_tensor(sq, hs[:, :, :], hs[:, :, :], ALU.mult))
            done(nc.vector.tensor_reduce(var[:, :], sq, AX.X, ALU.add))
            nc.vector.tensor_scalar(var[:, :], var[:, :], 1.0 / D, EPS, ALU.mult, ALU.add).then_inc(ln_var, 1)
            dve.wait_ge(ln_root, 1)
            done(nc.vector.reciprocal(rstd[:, :], std[:, :]))
            nc.vector.tensor_tensor(hs[:, :, :], hs[:, :, :], rstd[:, :, None].to_broadcast([P, T, D]), ALU.mult).then_inc(finished, 1)

        @block.gpsimd
        def _(pool):
            made = [0]

            def const(ins):
                made[0] += 1
                ins.then_inc(making, 1)
                pool.wait_ge(making, made[0])

            def keep(buffer, pattern, base, per_partition, compare=ALU.is_ge):
                const(nc.gpsimd.affine_select(out=buffer, in_=buffer, compare_op=compare, fill=0.0, base=base,
                                              pattern=pattern, channel_multiplier=per_partition))

            const(nc.gpsimd.memset(ones[:, :], 1.0))
            const(nc.gpsimd.memset(ones_b[:, :], 1.0))
            nc.gpsimd.affine_select(out=ident[:, :], in_=ones[:, :], compare_op=ALU.is_equal, fill=0.0, base=0,
                                    pattern=[[-1, P]], channel_multiplier=1).then_inc(consts, 1)
            const(nc.gpsimd.memset(not_own, 1.0))
            keep(not_own, [[1, T], [-1, T]], 0, 0, ALU.not_equal)
            const(nc.gpsimd.memset(before, 1.0))
            keep(before, [[1, P]], -1, -1)
            keep(before, [[-T, HALF], [0, T]], 0, 1)
            const(nc.gpsimd.memset(par4[:, :, :], 1.0))
            keep(par4[:, :, :], [[-T, 2], [-2 * T, 4]], 0, 1)
            keep(par4[:, :, :], [[T, 2], [2 * T, 4]], T - 1, -1)
            const(nc.gpsimd.tensor_tensor(par4[:, :, 0:2], par4[:, :, 0:2], par4[:, :, 2:4], ALU.add))
            const(nc.gpsimd.tensor_tensor(parity[:, :], par4[:, :, 0], par4[:, :, 1], ALU.add))
            exact = dict(allow_small_or_imprecise_dtypes=True)
            const(nc.gpsimd.iota(slot_no, [[1, SLOTS]], base=0, channel_multiplier=0, **exact))
            const(nc.gpsimd.iota(my_slot[:, :], [[0, T], [P, LISTS]], base=0, channel_multiplier=1, **exact))
            const(nc.gpsimd.iota(tile_base[:, :], [[0, 2], [T, HALF], [0, LISTS]], base=0, channel_multiplier=0, **exact))
            const(nc.gpsimd.iota(tile_row[:, :], [[N, T], [0, LISTS]], base=1, channel_multiplier=0, **exact))
            const(nc.gpsimd.memset(zero_row, 0.0))
            nc.gpsimd.iota(part_no[:, :], [[0, 1]], base=0, channel_multiplier=1, **exact).then_inc(consts, 1)
            pool.dma_start(at_dram[0:1, :], zero_row).then_inc(zero_stored, 16)
            pool.wait_ge(xw_out, 1)
            pool.dma_start(xw_dram.rearrange("(p t) f -> p t f", t=T), xw).then_inc(xw_stored, 16)
            pool.wait_ge(t01_ready, 1)
            nc.gpsimd.tensor_tensor(t0_ident[:, :], ident[:, :], t01[:, 0:1].to_broadcast([P, P]), ALU.mult).then_inc(making, 1)
            pool.wait_ge(making, made[0] + 1)
            steps = [0]

            def done(ins):
                steps[0] += 1
                ins.then_inc(listing, 1)
                pool.wait_ge(listing, steps[0])

            pool.wait_ge(local_ready, 1)
            done(nc.gpsimd.tensor_tensor(looked[:, :, 1], looked[:, :, 1], tile_base[:, :], ALU.subtract))
            pool.wait_ge(counted, 2 * T)
            done(nc.gpsimd.tensor_scalar(node[:, :], signs[:, :], T / 2.0, T * P / 2.0, ALU.mult, ALU.add))
            done(nc.gpsimd.tensor_tensor(node[:, :], node[:, :], looked[:, :, 1], ALU.add))
            done(nc.gpsimd.tensor_tensor(node_at[:, :], node[:, :], tile_row[:, :], ALU.add))
            done(nc.gpsimd.tensor_tensor(node_at[:, :], node_at[:, :], looked[:, :, 2], ALU.mult))
            done(nc.gpsimd.tensor_tensor(node[:, :], node[:, :], looked[:, :, 2], ALU.mult))
            nc.gpsimd.tensor_copy(lists[:, :, 0, :], node[:, :].rearrange("p (t q) -> p t q", t=T))
            nc.gpsimd.tensor_copy(lists[:, :, 1, :], node_at[:, :].rearrange("p (t q) -> p t q", t=T)).then_inc(lists_ready, 1)
            pool.wait_ge(resident, T)
            pool.wait_ge(col_summed, T)
            pool.wait_ge(lists_ready, 1)

            def gather(s, t):
                if not (isinstance(t, int) and t < 2):
                    pool.wait_ge(b_made, t - 1)
                nc.gpsimd.tensor_copy(list_now[s][:, :, :].rearrange("p a q -> p (a q)"),
                                      lists[:, bass.ds(t, 1), :, :].rearrange("p o a q -> p (o a q)")).then_inc(list_taken, 1)
                pool.wait_ge(zero_stored, 16)
                pool.wait_ge(at_stored[s], 16 * (t // 2 + 1) if isinstance(t, int) else 16 * HALF)
                pool.wait_ge(list_taken, t + 1)
                pool.nop(nofuse=True)
                for q in range(LISTS):
                    pool.indirect_dma_start(out=edge[s][:, q, :], out_offset=None, in_=at_dram[0:1 + N * (t + 1 if isinstance(t, int) else T), :],
                                            in_offset=bass.IndirectOffsetOnAxis(ap=list_now[s][:, 1, q:q + 1], axis=0)).then_inc(edges_in[s], 16)
                for q in range(LISTS):
                    pool.indirect_dma_start(out=rows[s][q][:, :], out_offset=None, in_=adj,
                                            in_offset=bass.IndirectOffsetOnAxis(ap=list_now[s][:, 0, q:q + 1], axis=0)).then_inc(rows_in[s][q], 16)
                pool.wait_ge(own_scaled, t + 1)
                nc.gpsimd.tensor_tensor(own[s][:, :], own_raw[s][:, :], t0_ident[:, :], ALU.add).then_inc(own_ready, 1)

            def pick(r, t):
                if not (isinstance(t, int) and t < PICKS):
                    pool.wait_ge(hs_ready, t - PICKS + 1)
                pool.wait_ge(xw_stored, 16)
                pool.wait_ge(idx_ready, t + 1)
                pool.nop(nofuse=True)
                for m in range(TOPK):
                    pool.indirect_dma_start(out=picked[r][:, m, :], out_offset=None, in_=xw_dram,
                                            in_offset=bass.IndirectOffsetOnAxis(ap=idx[r][:, m:m + 1], axis=0)).then_inc(picks_in[r], 16)

            def weigh_all(s, n, t):
                pool.wait_ge(all_in[s], 16 * n + 16)
                nc.gpsimd.tensor_tensor(all_edges[s], all_edges[s], w[:, :, None].to_broadcast([P, T, P]), ALU.mult).then_inc(all_scaled, 1)
                pool.wait_ge(all_scaled, t + 1)
                nc.gpsimd.tensor_tensor(tile_of(all_edges[s], t), tile_of(all_edges[s], t), t0_ident[:, :], ALU.add).then_inc(all_ready, 1)

            overflow = overflow_flag(pool)
            with pool.If(overflow == 0):
                for t in range(AHEAD):
                    gather(t % 2, t)
                for t in range(PICKS):
                    gather(t % 2, t + AHEAD)
                    pick(t, t)
                with pool.Fori(1, T // PICKS - 1) as i:
                    for j in range(PICKS):
                        gather(j % 2, PICKS * i + j + AHEAD)
                        pick(j, PICKS * i + j)
                for t in range(T - AHEAD, T):
                    pick(t % PICKS, t)
            with pool.Else():
                for t in range(PICKS + 2):
                    weigh_all(t % 2, t // 2, t)
                    if t >= 2:
                        pick(t - 2, t - 2)
                with pool.Fori(1, T // PICKS - 1) as i:
                    for j in range(PICKS):
                        weigh_all(j % 2, 2 * i + j // 2 + 1, PICKS * i + j + 2)
                        pick(j, PICKS * i + j)
                for t in range(T - PICKS, T):
                    if t + 2 < T:
                        weigh_all(t % 2, t // 2 + 1, t + 2)
                    pick(t % PICKS, t)


_INS = ["x", "adj", "L0_gnn_theta", "L0_gnn_W", "L0_gnn_b"]


def kernel(**inputs):
    import numpy as _np
    import concourse.bacc as _bacc
    from concourse import mybir as _mybir
    from concourse.bass_utils import run_bass_kernel_spmd as _run

    nc = _bacc.Bacc("TRN2", target_bir_lowering=False, num_devices=1)
    arrays, args = {}, []
    for name in _INS:
        a = _np.ascontiguousarray(inputs[name])
        arrays[f"in_{name}_dram"] = a
        args.append(nc.dram_tensor(f"in_{name}_dram", a.shape, _mybir.dt.from_np(a.dtype), kind="ExternalInput").ap())
    out = nc.dram_tensor("out_0_dram", inputs["x"].shape, _mybir.dt.float32, kind="ExternalOutput").ap()
    adjacency_resnorm(nc, *args, out)
    r = _run(nc, [arrays], core_ids=[0])
    return r.results[0]["out_0_dram"]
```

```python
import concourse.bass as bass
from concourse import mybir
from contextlib import ExitStack


def adjacency_resnorm(nc, x, adj, theta, W, b, out):
    fp32 = mybir.dt.float32
    fp16 = mybir.dt.float16
    bf16 = mybir.dt.bfloat16
    u32 = mybir.dt.uint32
    ALU = mybir.AluOpType
    ACT = mybir.ActivationFunctionType
    AX = mybir.AxisListType

    P = 128
    N = adj.shape[0]
    D = x.shape[1]
    T = N // P
    BANK = 512
    NB = N // BANK
    TOPK = 4
    EPS = 1e-5
    LISTS = 2
    SLOTS = LISTS * P
    HALF = T // 2
    LOOK = 3
    STAGES = 4
    PICKS = 4
    AHEAD = 4
    LOOKED_AT = 384
    SUMS_AT = 3 * BANK
    LAG = 3
    BETWEEN = 5
    FIRST_B = 9
    WITH_B = ((9, 10), (11, 12))
    SECOND_B = 13
    HOLD = 9
    AT_RING = 3
    EARLY = 2
    FIRST = 3

    with ExitStack() as ctx:
        def sb(name, shape, dt=fp32):
            return ctx.enter_context(nc.sbuf_tensor(name, shape, dt))

        def sem(name):
            return ctx.enter_context(nc.semaphore(name))

        at_dram = nc.dram_tensor("at_dram", [T * N + 1, P + 1], fp32, kind="Internal").ap()
        at_tiles = at_dram[1:, :].rearrange("(t p j) i -> t p j i", t=T, j=T)
        xw_dram = nc.dram_tensor("xw_dram", [N, D], fp32, kind="Internal").ap()
        vec_dram = [nc.dram_tensor(f"vec_dram{n}", [P, T], fp32, kind="Internal").ap() for n in range(3)]

        b_dram = nc.dram_tensor("b_dram", [T, P, N], fp32, kind="Internal").ap()

        A = sb("A", [P, T, N])
        big = [sb(f"big{n}", [P, N]) for n in range(STAGES - 1)]
        last_big = sb("last_big", [P, T, P + 1])
        big.append(last_big[:, :, :].rearrange("p j i -> p (j i)")[:, 0:N])
        stage = big
        rows = [big[0:2], big[2:4]]
        at = [sb(f"at{s}", [P, T, P + 1]) for s in range(2)] + [last_big]
        G = [at[s][:, :, :].rearrange("p j i -> p (j i)")[:, 0:N] for s in range(2)]
        b_stage = [big[1], big[3]]
        b_back = [big[0], big[2]]
        all_edges = [big[2 * s][:, :].rearrange("p (j i) -> p j i", j=T) for s in range(2)]
        vec = sb("vec", [P, N])
        junk = sb("junk", [P, N], bf16)
        ident = sb("ident", [P, P])
        t0_ident = sb("t0_ident", [P, P])
        ones = sb("ones", [P, P])
        ones_b = sb("ones_b", [P, 1], bf16)
        my_slot = sb("my_slot", [P, 2 * T])
        tile_base = sb("tile_base", [P, 2 * T])
        tile_row = sb("tile_row", [P, 2 * T])
        part_no = sb("part_no", [P, 1])
        par4 = sb("par4", [P, 2, 4])
        parity = sb("parity", [P, 2])
        count = sb("count", [P, 2])
        prefix = sb("prefix", [P, 2, P + LOOK], fp16)
        start = sb("start", [P, 2])
        end = sb("end", [P, 2])
        over = sb("over", [P, 2])
        over_sum = sb("over_sum", [P, 1])
        flag = sb("flag", [P, 1], u32)
        looked = sb("looked", [P, 2 * T, LOOK])
        local = sb("local", [P, 2 * T])
        signs = sb("signs", [P, 2 * T])
        node = sb("node", [P, 2 * T])
        node_at = sb("node_at", [P, 2 * T])
        lists = sb("lists", [P, T, 2, LISTS], u32)
        list_now = [sb(f"list_now{s}", [P, 2, LISTS], u32) for s in range(2)]
        t01 = sb("t01", [P, 2])
        d = sb("d", [P, T])
        root = sb("root", [P, T])
        y = sb("y", [P, T])
        tmp = sb("tmp", [P, T])
        tmp2 = sb("tmp2", [P, T])
        y2 = sb("y2", [P, T])
        w = sb("w", [P, T])
        r1 = sb("r1", [P, T])
        v = sb("v", [P, T])
        r2 = sb("r2", [P, T])
        d2 = sb("d2", [P, T])
        c = sb("c", [P, T])
        dc = sb("dc", [P, T])
        hs = sb("hs", [P, T, D])
        Ws = sb("Ws", [D, D])
        WT = sb("WT", [D, D])
        b_all = sb("b_all", [P, D])
        edge = [sb(f"edge{s}", [P, LISTS, P + 1]) for s in range(2)]
        own_raw = [sb(f"own_raw{s}", [P, P]) for s in range(2)]
        own = [sb(f"own{s}", [P, P]) for s in range(2)]
        top = [sb(f"top{s}", [P, 8]) for s in range(PICKS)]
        idx = [sb(f"idx{s}", [P, 8], u32) for s in range(PICKS)]
        coef = [sb(f"coef{s}", [P, 8]) for s in range(PICKS)]
        all_picked = sb("all_picked", [P, PICKS, TOPK, D])
        picked = [all_picked[:, s] for s in range(PICKS)]
        junks = [junk[:, :], all_picked[:, :, :, :].rearrange("p s m f -> p (s m f)").bitcast(bf16)[:, 0:N]]
        mean = sb("mean", [P, T])
        var = sb("var", [P, T])
        std = sb("std", [P, T])
        rstd = sb("rstd", [P, T])
        xT = G[1][0:D, :].rearrange("f (t p) -> f t p", t=T)
        xw = vec[:, 0:T * D].rearrange("p (t f) -> p t f", t=T)
        not_own = picked[0][:, :, :].rearrange("p m f -> p (m f)").rearrange("p (t j) -> p t j", t=T)
        before = picked[1][:, 0:2, :].rearrange("p m f -> p (m f)")
        slot_no = picked[2][:, :, :].rearrange("p m f -> p (m f)")
        zero_row = picked[3][:, :, :].rearrange("p m f -> p (m f)")[0:1, 0:P + 1]
        mask = big[0][:, 0:T * T].rearrange("p (t j) -> p t j", t=T)
        past = big[0][:, BANK:BANK + 2 * SLOTS].rearrange("p (h s) -> p h s", h=2)
        inside = big[0][:, 2 * BANK:2 * BANK + 2 * SLOTS].rearrange("p (h s) -> p h s", h=2)
        pick_block = big[2][:, 0:2 * SLOTS].bitcast(fp16).rearrange("p (h r s) -> p h r s", h=2, r=2)
        sign_out = big[2][:, N // 2:N].bitcast(bf16)
        sq = big[0][:, 0:T * D].rearrange("p (t f) -> p t f", t=T)

        ps = [ctx.enter_context(nc.psum_tensor(f"ps{s}", [P, N], fp32)) for s in range(2)]

        small_in = sem("small_in")
        consts = sem("consts")
        making = sem("making")
        t01_ready = sem("t01_ready")
        d2_ready = sem("d2_ready")
        x_turned = sem("x_turned")
        x_turned_out = sem("x_turned_out")
        xw_made = sem("xw_made")
        xw_out = sem("xw_out")
        xw_stored = sem("xw_stored")
        zero_stored = sem("zero_stored")
        loaded = [sem(f"loaded{s}") for s in range(STAGES)]
        resident = sem("resident")
        turned = sem("turned")
        turned_out = sem("turned_out")
        col_summed = sem("col_summed")
        w_placed = sem("w_placed")
        at_stored = [sem(f"at_stored{r}") for r in range(AT_RING)]
        rooted = sem("rooted")
        step = sem("step")
        col_ready = sem("col_ready")
        w_ready = sem("w_ready")
        vec_stored = [sem(f"vec_stored{n}") for n in range(3)]
        vec_spread = [sem(f"vec_spread{n}") for n in range(3)]
        mask_ready = sem("mask_ready")
        mask_turned = sem("mask_turned")
        prefix_ready = sem("prefix_ready")
        start_made = sem("start_made")
        over_ready = sem("over_ready")
        over_made = sem("over_made")
        flag_ready = sem("flag_ready")
        blocks_ready = sem("blocks_ready")
        looked_made = sem("looked_made")
        prefix_made = sem("prefix_made")
        local_ready = sem("local_ready")
        counted = sem("counted")
        listing = sem("listing")
        lists_ready = sem("lists_ready")
        list_taken = sem("list_taken")
        edges_in = [sem(f"edges_in{s}") for s in range(2)]
        rows_in = [[sem(f"rows_in{s}{q}") for q in range(LISTS)] for s in range(2)]
        own_in = [sem(f"own_in{s}") for s in range(2)]
        edges_ready = sem("edges_ready")
        all_in = [sem(f"all_in{s}") for s in range(2)]
        all_scaled = sem("all_scaled")
        all_ready = sem("all_ready")
        all_made = sem("all_made")
        all_out = sem("all_out")
        b_stored = [sem(f"b_stored{s}") for s in range(2)]
        b_back_in = [sem(f"b_back_in{s}") for s in range(2)]
        own_scaled = sem("own_scaled")
        own_ready = sem("own_ready")
        b_made = sem("b_made")
        b_out = sem("b_out")
        last_made = sem("last_made")
        pass1 = sem("pass1")
        pass2 = sem("pass2")
        g_scaled = sem("g_scaled")
        g_ready = sem("g_ready")
        top_ready = sem("top_ready")
        idx_ready = sem("idx_ready")
        coef_ready = sem("coef_ready")
        picks_in = [sem(f"picks_in{s}") for s in range(PICKS)]
        weighted = sem("weighted")
        pairs = sem("pairs")
        summed = sem("summed")
        hs_ready = sem("hs_ready")
        ln_var = sem("ln_var")
        ln_root = sem("ln_root")
        finished = sem("finished")
        out_stored = sem("out_stored")

        def tile_of(buffer3, t):
            return buffer3[:, bass.ds(t, 1), :].rearrange("p o f -> p (o f)")

        def wait_stored(engine, t):
            engine.wait_ge(at_stored[t % AT_RING], 16 * (t // AT_RING + 1))

        def wait_free(engine, r, t=T):
            wait_stored(engine, max(range(r, t, AT_RING)))

        def wait_all_stored(engine):
            for r in range(AT_RING):
                wait_free(engine, r)

        def overflow_flag(engine):
            engine.wait_ge(flag_ready, 1)
            return engine.value_load(flag[0:1, 0:1])

        block = ctx.enter_context(nc.Block())

        @block.sync
        def _(sp):
            adj_tiles = adj.rearrange("(p t) k -> t p k", t=T)
            for s in range(STAGES):
                sp.dma_start(stage[s][:, :], adj_tiles[s]).then_inc(loaded[s], 16)
            with sp.Fori(1, T // STAGES) as i:
                for s in range(STAGES):
                    sp.wait_ge(resident, STAGES * (i - 1) + s + 1)
                    sp.wait_ge(col_summed, STAGES * (i - 1) + s + 1)
                    sp.dma_start(stage[s][:, :], adj_tiles[bass.ds(STAGES * i + s, 1)].rearrange("o p k -> p (o k)")).then_inc(loaded[s], 16)
            sp.wait_ge(col_ready, 1)
            sp.wait_ge(xw_stored, 16)
            sp.dma_start(vec_dram[0], y[:, :]).then_inc(vec_stored[0], 16)
            sp.wait_ge(vec_stored[0], 16)
            sp.dma_start(vec[:, :], vec_dram[0].rearrange("p t -> (p t)").rearrange("(o k) -> o k", o=1).to_broadcast([P, N])).then_inc(vec_spread[0], 16)
            def spread(n, vector):
                sp.wait_ge(col_ready, n + 1)
                sp.dma_start(vec_dram[n], vector[:, :]).then_inc(vec_stored[n], 16)
                sp.wait_ge(vec_stored[n], 16)
                sp.dma_start(vec[:, :], vec_dram[n].rearrange("p t -> (p t)").rearrange("(o k) -> o k", o=1).to_broadcast([P, N])).then_inc(vec_spread[n], 16)

            def own_rows(s, t):
                sp.dma_start(own_raw[s][:, :], at_tiles[bass.ds(t, 1), :, bass.ds(t, 1), 0:P].rearrange("a p b i -> p (a b i)")).then_inc(own_in[s], 16)

            def all_rows(s, t):
                sp.dma_start(all_edges[s], at_tiles[bass.ds(t, 1), :, :, 0:P].rearrange("o p j i -> p (o j) i")).then_inc(all_in[s], 16)

            overflow = overflow_flag(sp)
            with sp.If(overflow == 0):
                for s in range(2):
                    wait_stored(sp, s)
                    own_rows(s, s)
                spread(1, v)
                for s in range(2):
                    sp.wait_ge(own_ready, s + 1)
                    wait_stored(sp, s + 2)
                    own_rows(s, s + 2)
                spread(2, c)
                wait_all_stored(sp)
                with sp.Fori(2, T // 2) as i:
                    for s in range(2):
                        sp.wait_ge(own_ready, 2 * i + s - 1)
                        own_rows(s, 2 * i + s)
            with sp.Else():
                spread(1, v)
                sp.wait_ge(lists_ready, 2)
                sp.wait_ge(counted, 2 * T)
                sp.wait_ge(resident, T)
                sp.wait_ge(col_summed, T)
                wait_all_stored(sp)
                for s in range(2):
                    all_rows(s, s)
                spread(2, c)
                with sp.Fori(1, T // 2) as i:
                    for s in range(2):
                        sp.wait_ge(all_made, 2 * i + s - 1)
                        all_rows(s, 2 * i + s)

                def bring_back(s, t):
                    sp.dma_start(b_back[s][:, :], b_dram[bass.ds(t, 1)].rearrange("o p k -> (o p) k")).then_inc(b_back_in[s], 16)

                sp.wait_ge(all_made, T)
                for s in range(2):
                    sp.wait_ge(b_stored[s], 16 * HALF)
                for s in range(2):
                    bring_back(s, s)
                with sp.Fori(1, T // 2) as i:
                    for s in range(2):
                        sp.wait_ge(b_out, 2 * i + s - 1)
                        bring_back(s, 2 * i + s)
            for n, tiles in enumerate((slice(0, T - 1), slice(T - 1, T))):
                sp.wait_ge(finished, n + 1)
                sp.dma_start(out.rearrange("(p t) f -> p t f", t=T)[:, tiles, :], hs[:, tiles, :]).then_inc(out_stored, 16)
            sp.wait_ge(out_stored, 32)

        @block.scalar
        def _(act):
            act.dma_start(hs[:, :, :], x.rearrange("(p t) f -> p t f", t=T)).then_inc(small_in, 16)
            act.dma_start(Ws[:, :], W).then_inc(small_in, 16)
            act.dma_start(t01[:, :], theta.rearrange("(o k) -> o k", o=1).to_broadcast([P, 2])).then_inc(small_in, 16)
            act.dma_start(b_all[:, :], b.rearrange("(o k) -> o k", o=1).to_broadcast([P, D])).then_inc(small_in, 16)

            def keep_tile(s, i):
                act.wait_ge(loaded[s], 16 * i + 16)
                nc.scalar.activation(tile_of(A, STAGES * i + s), stage[s][:, :], ACT.Copy,
                                     accum_out=d[:, bass.ds(STAGES * i + s, 1)]).then_inc(resident, 1)

            for s in range(STAGES):
                keep_tile(s, 0)
            act.wait_ge(small_in, 64)
            nc.scalar.activation(t01[:, :], t01[:, :], ACT.Sigmoid).then_inc(t01_ready, 1)
            with act.Fori(1, T // STAGES) as i:
                for s in range(STAGES):
                    keep_tile(s, i)
            act.wait_ge(resident, T)
            nc.scalar.activation(root[:, :], d[:, :], ACT.Sqrt).then_inc(rooted, 1)

            def take_turned(t):
                r = t % AT_RING
                room = ps[0] if t < FIRST else ps[1]
                for h in range(2):
                    act.wait_ge(turned, 2 * t + h + 1)
                    if h == 0 and t >= AT_RING:
                        wait_free(act, r, t)
                    nc.scalar.activation(at[r][:, h * HALF:(h + 1) * HALF, 0:P],
                                         room[:, h * 2 * BANK:(h + 1) * 2 * BANK].rearrange("p (j i) -> p j i", j=HALF),
                                         ACT.Copy).then_inc(turned_out, 1)
                if t >= FIRST:
                    store_turned(t)

            def store_turned(t):
                r = t % AT_RING
                if t < AT_RING:
                    act.wait_ge(w_ready, 1)
                    nc.scalar.activation(at[r][:, :, P], w[:, :], ACT.Copy).then_inc(w_placed, 1)
                    act.wait_ge(w_placed, t + 1)
                if t == HOLD:
                    act.wait_ge(vec_stored[1], 16)
                act.wait_ge(turned_out, 2 * t + 2)
                act.dma_start(at_tiles[t], at[r][:, :, :]).then_inc(at_stored[r], 16)

            for t in range(EARLY, FIRST):
                take_turned(t)
            act.wait_ge(vec_stored[0], 16)
            for t in range(FIRST):
                store_turned(t)
            act.wait_ge(local_ready, 1)
            for h in range(2):
                act.wait_ge(prefix_made, h + 1)
                for n in range(T):
                    nc.scalar.activation(sign_out[:, n * P:(n + 1) * P], ps[0][:, n * P:(n + 1) * P], ACT.Sign, scale=-1.0,
                                         bias=local[:, n + h * T:n + h * T + 1],
                                         accum_out=signs[:, n + h * T:n + h * T + 1]).then_inc(counted, 1)
                if h == 0:
                    for t in range(FIRST, BETWEEN):
                        take_turned(t)
                    act.wait_ge(counted, T)

            def edges(s, n, t):
                act.wait_ge(own_in[s], 16 * n + 16)
                nc.scalar.activation(own_raw[s][:, :], own_raw[s][:, :], ACT.Copy,
                                     scale=w[:, bass.ds(t, 1)]).then_inc(own_scaled, 1)
                act.wait_ge(edges_in[s], 32 * n + 32)
                for q in range(LISTS):
                    last = nc.scalar.activation(edge[s][:, q, 0:P], edge[s][:, q, 0:P], ACT.Copy, scale=edge[s][:, q, P:P + 1])
                last.then_inc(edges_ready, 1)

            def place_of(t):
                if isinstance(t, int) and t < 2:
                    wait_all_stored(act)
                    return G[t]
                if isinstance(t, int):
                    act.wait_ge(pass2, T)
                return tile_of(A, t)

            def take_b(s, t):
                act.wait_ge(b_made, t + 1)
                nc.scalar.activation(place_of(t), ps[s][:, :], ACT.Copy).then_inc(b_out, 1)

            def weigh(r, n, t):
                act.wait_ge(picks_in[r], 16 * TOPK * (n + 1))
                act.wait_ge(coef_ready, t + 1)
                for m in range(TOPK):
                    last = nc.scalar.activation(picked[r][:, m, :], picked[r][:, m, :], ACT.Copy, scale=coef[r][:, m:m + 1])
                last.then_inc(weighted, 1)

            def root_d2():
                act.wait_ge(d2_ready, 1)
                nc.scalar.activation(root[:, :], d2[:, :], ACT.Sqrt).then_inc(rooted, 1)

            overflow = overflow_flag(act)
            with act.If(overflow == 0):
                for t in range(BETWEEN, T):
                    take_turned(t)
                    if t + 1 == FIRST_B:
                        edges(0, 0, 0)
                    if t == SECOND_B:
                        edges(1, 0, 1)
                take_b(0, 0)
                edges(0, 1, 2)
                take_b(1, 1)
                edges(1, 1, 3)
                root_d2()
                take_b(0, 2)
                edges(0, 2, 4)
                for t in range(LAG, LAG + 2):
                    take_b(t % 2, t)
                    edges(t % 2, t // 2 + 1, t + 2)
                    weigh(t - LAG, 0, t - LAG)
                with act.Fori(0, 2) as i:
                    for j in range(PICKS):
                        s = (LAG + 2 + j) % 2
                        take_b(s, 4 * i + LAG + 2 + j)
                        edges(s, 2 * i + (LAG + 2 + j) // 2 + 1, 4 * i + LAG + 4 + j)
                        weigh((2 + j) % PICKS, i + (2 + j) // PICKS, 4 * i + 2 + j)
                for t in range(T - LAG, T + LAG):
                    if t < T - 1:
                        take_b(t % 2, t)
                    if t + 2 < T:
                        edges(t % 2, t // 2 + 1, t + 2)
                    weigh((t - LAG) % PICKS, (t - LAG) // PICKS, t - LAG)
            with act.Else():
                def take_all(s, i):
                    t = 2 * i + s
                    act.wait_ge(all_made, t + 1)
                    if not isinstance(i, int):
                        act.wait_ge(b_stored[s], 16 * i)
                    nc.scalar.activation(b_stage[s][:, :], ps[s][:, :], ACT.Copy).then_inc(all_out, 1)
                    act.wait_ge(all_out, t + 1)
                    act.dma_start(b_dram[bass.ds(t, 1)].rearrange("o p k -> (o p) k"), b_stage[s][:, :]).then_inc(b_stored[s], 16)

                def take_back(s, n, t, place=None, signal=b_out):
                    act.wait_ge(b_back_in[s], 16 * n + 16)
                    nc.scalar.activation(place_of(t) if place is None else place, b_back[s][:, :], ACT.Copy).then_inc(signal, 1)

                for t in range(BETWEEN, T):
                    take_turned(t)
                wait_all_stored(act)
                root_d2()
                for s in range(2):
                    take_all(s, 0)
                with act.Fori(1, T // 2) as i:
                    for s in range(2):
                        take_all(s, i)
                for t in range(PICKS):
                    take_back(t % 2, t // 2, t)
                    if t >= LAG:
                        weigh(t - LAG, 0, t - LAG)
                with act.Fori(1, T // PICKS - 1) as i:
                    for j in range(PICKS):
                        take_back(j % 2, 2 * i + j // 2, 4 * i + j)
                        weigh((j + 1) % PICKS, i - 1 + (j + 1) // PICKS, 4 * i + j - LAG)
                for t in range(T - PICKS, T):
                    if t < T - 1:
                        take_back(t % 2, t // 2, t)
                    else:
                        take_back(1, t // 2, t, ps[1][:, :], last_made)
                    weigh((t - LAG) % PICKS, (t - LAG) // PICKS, t - LAG)
                for t in range(T - LAG, T):
                    weigh(t % PICKS, t // PICKS, t)
            for n, tiles in enumerate((slice(0, T - 1), slice(T - 1, T))):
                act.wait_ge(ln_var, n + 1)
                nc.scalar.activation(std[:, tiles], var[:, tiles], ACT.Sqrt).then_inc(ln_root, 1)

        @block.tensor
        def _(pe):
            pe.wait_ge(consts, 1)
            def column_sums(s, i):
                upper = stage[s][:, :].bitcast(bf16)[:, 1:2 * N:2]
                pe.wait_ge(loaded[s], 16 * i + 16)
                for j in range(T):
                    mm = nc.tensor.matmul(ps[1][:, bass.ds(SUMS_AT + (STAGES * i + s) * T + j, 1)], upper[:, j:N:T], ones_b[:, :],
                                          start=True, stop=True, skip_group_check=True)
                mm.then_inc(col_summed, 1)

            for s in range(STAGES):
                column_sums(s, 0)
            pe.wait_ge(small_in, 64)
            for t in range(T):
                nc.tensor.transpose(ps[0][0:D, t * P:(t + 1) * P], hs[:, t, :], ident[:, :])
            nc.tensor.transpose(ps[1][0:D, 0:D], Ws[:, :], ident[0:D, 0:D]).then_inc(x_turned, 1)
            column_sums(0, 1)
            column_sums(1, 1)
            pe.wait_ge(x_turned_out, 1)
            for t in range(T):
                mm = nc.tensor.matmul(ps[1][:, t * D:(t + 1) * D], xT[:, t, :], WT[:, :], start=True, stop=True)
            mm.then_inc(xw_made, 1)
            column_sums(2, 1)
            column_sums(3, 1)
            for s in range(STAGES):
                column_sums(s, 2)

            def turn(t):
                pe.wait_ge(resident, T if t >= EARLY else STAGES)
                room = ps[0] if t < FIRST else ps[1]
                for h in range(2):
                    if t not in (0, FIRST):
                        pe.wait_ge(turned_out, 2 * t + h - 1)
                    for j in range(h * HALF, (h + 1) * HALF):
                        mm = nc.tensor.transpose(room[:, j * P:(j + 1) * P], A[:, t, j:N:T], ident[:, :])
                    mm.then_inc(turned, 1)

            for t in range(EARLY):
                turn(t)
            with pe.Fori(3, T // STAGES) as i:
                for s in range(STAGES):
                    column_sums(s, i)
            pe.wait_ge(xw_out, 1)
            pe.wait_ge(mask_ready, 1)
            for h in range(2):
                mm = nc.tensor.transpose(ps[1][:, BANK + h * P:BANK + (h + 1) * P],
                                         mask[:, h * HALF:(h + 1) * HALF, :].rearrange("p t j -> p (t j)"), ident[:, :])
            mm.then_inc(mask_turned, 1)
            turn(2)
            pe.wait_ge(prefix_ready, 1)
            nc.tensor.matmul(ps[1][:, 2 * BANK:2 * BANK + 2], before, count[:, :], start=True, stop=True).then_inc(start_made, 1)
            pe.wait_ge(over_ready, 1)
            nc.tensor.matmul(ps[1][:, 2 * BANK + 8:2 * BANK + 10], ones[:, :], over[:, :], start=True, stop=True).then_inc(over_made, 1)
            pe.wait_ge(blocks_ready, 1)
            pe.wait_ge(flag_ready, 1)
            for t in range(T):
                h, g, r = t // HALF, (t % HALF) // 2, t % 2
                k = slice(32 * g, 32 * g + 32)
                for q in range(LISTS):
                    at = g * BANK + LOOKED_AT + ((h * 2 + r) * LISTS + q) * LOOK
                    mm = nc.tensor.matmul(ps[1][:, at:at + LOOK], pick_block[k, h, r, q * P:(q + 1) * P],
                                          prefix[k, h, P:P + LOOK], start=True, stop=True, skip_group_check=True)
            mm.then_inc(looked_made, 1)
            for h in range(2):
                if h == 1:
                    pe.wait_ge(counted, T)
                else:
                    pe.wait_ge(turned_out, 2 * FIRST)
                for t in range(HALF):
                    g, r = t // 2, t % 2
                    k = slice(32 * g, 32 * g + 32)
                    for q in range(LISTS):
                        at = (t * LISTS + q) * P
                        mm = nc.tensor.matmul(ps[0][:, at:at + P], pick_block[k, h, r, q * P:(q + 1) * P],
                                              prefix[k, h, 0:P], start=True, stop=True, skip_group_check=True)
                mm.then_inc(prefix_made, 1)
                if h == 0:
                    pe.wait_ge(local_ready, 1)
                    for t in range(FIRST, BETWEEN):
                        turn(t)

            def product(s, n, t, between=(), signal=b_made):
                pe.wait_ge(own_ready, t + 1)
                pe.wait_ge(edges_ready, t + 1)
                if isinstance(t, int) and t == 0:
                    pe.wait_ge(counted, 2 * T)
                elif isinstance(t, int) and t == 1:
                    pe.wait_ge(turned_out, 2 * T)
                else:
                    pe.wait_ge(b_out, t - 1)
                for k in range(LISTS + 1):
                    if k:
                        for other in between[k - 1] if between else ():
                            turn(other)
                        pe.wait_ge(rows_in[s][k - 1], 16 * n + 16)
                    for m in range(NB):
                        cols = slice(m * BANK, (m + 1) * BANK)
                        if k:
                            mm = nc.tensor.matmul(ps[s][:, cols], edge[s][:, k - 1, 0:P], rows[s][k - 1][:, cols],
                                                  start=False, stop=(k == LISTS), skip_group_check=True)
                        else:
                            mm = nc.tensor.matmul(ps[s][:, cols], own[s][:, :],
                                                  A[:, bass.ds(t, 1), cols].rearrange("p o k -> p (o k)"),
                                                  start=True, stop=False, skip_group_check=True)
                mm.then_inc(signal, 1)

            def product_of_all(s, t):
                pe.wait_ge(all_ready, t + 1)
                if isinstance(t, int) and t == 0:
                    pe.wait_ge(counted, 2 * T)
                elif isinstance(t, int) and t == 1:
                    pe.wait_ge(turned_out, 2 * T)
                else:
                    pe.wait_ge(all_out, t - 1)
                for j in range(T):
                    for m in range(NB):
                        cols = slice(m * BANK, (m + 1) * BANK)
                        mm = nc.tensor.matmul(ps[s][:, cols], all_edges[s][:, j, :], A[:, j, cols],
                                              start=(j == 0), stop=(j == T - 1), skip_group_check=True)
                mm.then_inc(all_made, 1)

            overflow = overflow_flag(pe)
            with pe.If(overflow == 0):
                for t in range(BETWEEN, FIRST_B):
                    turn(t)
                product(0, 0, 0, between=WITH_B)
                for t in range(WITH_B[1][-1] + 1, T):
                    turn(t)
                product(1, 0, 1)
                with pe.Fori(1, T // 2 - 1) as i:
                    for s in range(2):
                        product(s, i, 2 * i + s)
                product(0, T // 2 - 1, T - 2)
                product(1, T // 2 - 1, T - 1, signal=last_made)
            with pe.Else():
                for t in range(BETWEEN, T):
                    turn(t)
                product_of_all(0, 0)
                product_of_all(1, 1)
                with pe.Fori(1, T // 2) as i:
                    for s in range(2):
                        product_of_all(s, 2 * i + s)

        @block.vector
        def _(dve):
            chain = [0]

            def done(ins):
                chain[0] += 1
                ins.then_inc(step, 1)
                dve.wait_ge(step, chain[0])

            dve.wait_ge(x_turned, 1)
            nc.vector.tensor_copy(xT[:, :, :], ps[0][0:D, :].rearrange("f (t p) -> f t p", t=T))
            nc.vector.tensor_copy(WT[:, :], ps[1][0:D, 0:D]).then_inc(x_turned_out, 1)
            nc.vector.tensor_tensor(hs[:, :, :], hs[:, :, :], b_all[:, None, :].to_broadcast([P, T, D]), ALU.add)
            dve.wait_ge(xw_made, 1)
            nc.vector.tensor_copy(xw, ps[1][:, 0:T * D].rearrange("p (t f) -> p t f", t=T)).then_inc(xw_out, 1)

            for t in range(EARLY):
                for h in range(2):
                    dve.wait_ge(turned, 2 * t + h + 1)
                    nc.vector.tensor_copy(at[t][:, h * HALF:(h + 1) * HALF, 0:P],
                                          ps[0][:, h * 2 * BANK:(h + 1) * 2 * BANK].rearrange("p (j i) -> p j i", j=HALF)
                                          ).then_inc(turned_out, 1)

            def inverse_root(dst, src):
                done(nc.vector.reciprocal(tmp[:, :], root[:, :]))
                done(nc.vector.tensor_tensor(tmp2[:, :], tmp[:, :], tmp[:, :], ALU.mult))
                done(nc.vector.tensor_tensor(tmp2[:, :], tmp2[:, :], src[:, :], ALU.mult))
                done(nc.vector.tensor_scalar(tmp2[:, :], tmp2[:, :], -0.5, 1.5, ALU.mult, ALU.add))
                done(nc.vector.tensor_tensor(dst[:, :], tmp[:, :], tmp2[:, :], ALU.mult))

            dve.wait_ge(col_summed, T)
            dve.wait_ge(consts, 2)
            dve.wait_ge(resident, T)
            nc.vector.scalar_tensor_tensor(out=mask, in0=ps[1][:, SUMS_AT:SUMS_AT + T * T].rearrange("p (t j) -> p t j", t=T), scalar=0.0,
                                           in1=not_own, op0=ALU.not_equal, op1=ALU.mult).then_inc(mask_ready, 1)
            dve.wait_ge(rooted, 1)
            inverse_root(y, d)
            nc.vector.tensor_tensor(y2[:, :], y[:, :], y[:, :], ALU.mult).then_inc(col_ready, 1)
            dve.wait_ge(mask_turned, 1)
            for h in range(2):
                done(nc.vector.tensor_tensor_scan(out=prefix[:, h, 0:P], data0=ones[:, :], data1=ps[1][:, BANK + h * P:BANK + (h + 1) * P],
                                                  initial=0.0, op0=ALU.mult, op1=ALU.add))
            nc.vector.tensor_copy(count[:, :], prefix[:, :, P - 1]).then_inc(prefix_ready, 1)
            dve.wait_ge(t01_ready, 1)
            nc.vector.tensor_scalar(w[:, :], y2[:, :], t01[:, 1:2], None, ALU.mult).then_inc(w_ready, 1)
            dve.wait_ge(start_made, 1)
            done(nc.vector.tensor_copy(start[:, :], ps[1][:, 2 * BANK:2 * BANK + 2]))
            done(nc.vector.tensor_tensor(end[:, :], start[:, :], count[:, :], ALU.add))
            nc.vector.tensor_scalar(over[:, :], end[:, :], float(SLOTS), None, ALU.is_gt).then_inc(over_ready, 1)
            for h in range(2):
                nc.vector.tensor_copy(prefix[:, h, P:P + 1], start[:, h:h + 1])
                nc.vector.tensor_copy(prefix[:, h, P + 1:P + 2], part_no[:, :])
                nc.vector.memset(prefix[:, h, P + 2:P + 3], 1.0)
                done(nc.vector.tensor_scalar(past[:, h, :], slot_no, end[:, h:h + 1], None, ALU.is_ge))
                done(nc.vector.scalar_tensor_tensor(out=inside[:, h, :], in0=slot_no, scalar=start[:, h:h + 1],
                                                    in1=past[:, h, :], op0=ALU.is_ge, op1=ALU.subtract))
                for r in range(2):
                    last = nc.vector.tensor_scalar(pick_block[:, h, r, :], inside[:, h, :], parity[:, r:r + 1], None, ALU.mult)
            last.then_inc(blocks_ready, 1)
            dve.wait_ge(over_made, 1)
            done(nc.vector.tensor_reduce(over_sum[:, :], ps[1][:, 2 * BANK + 8:2 * BANK + 10], AX.X, ALU.add))
            nc.vector.tensor_copy(flag[:, :], over_sum[:, :]).then_inc(flag_ready, 1)
            dve.wait_ge(looked_made, 1)
            banks = ps[1][:, :].rearrange("p (g n) -> p g n", g=NB)[:, :, LOOKED_AT:LOOKED_AT + 4 * LISTS * LOOK]
            looked_v = looked[:, :, :].rearrange("p (h g rq) l -> p h g rq l", h=2, g=NB)
            for h in range(2):
                last = nc.vector.tensor_copy(looked_v[:, h], banks.rearrange("p g (h rq l) -> p h g rq l", h=2, l=LOOK)[:, h])
            done(last)
            done(nc.vector.tensor_tensor(local[:, :], my_slot[:, :], looked[:, :, 0], ALU.subtract))
            nc.vector.tensor_scalar(local[:, :], local[:, :], 0.5, None, ALU.add).then_inc(local_ready, 1)
            for n, (result, passed) in enumerate(((r1, pass1), (r2, pass2))):
                dve.wait_ge(vec_spread[n], 16)
                dve.wait_ge(zero_stored, 16)
                def row_sums(t):
                    nc.vector.scalar_tensor_tensor(out=junks[t % 2], in0=A[:, t, :], scalar=1.0, in1=vec[:, :],
                                                   op0=ALU.mult, op1=ALU.mult, accum_out=result[:, t:t + 1]).then_inc(passed, 1)

                for t in range(T):
                    if t >= 2:
                        dve.wait_ge(passed, t - 1)
                    row_sums(t)
                if n == 0:
                    dve.wait_ge(pass1, T)
                    done(nc.vector.tensor_tensor(v[:, :], y2[:, :], r1[:, :], ALU.mult))
                    nc.vector.tensor_scalar(tmp[:, :], r1[:, :], t01[:, 0:1], None, ALU.mult).then_inc(col_ready, 1)
            dve.wait_ge(pass2, T)
            dve.wait_ge(col_ready, 2)
            done(nc.vector.scalar_tensor_tensor(out=tmp2[:, :], in0=r2[:, :], scalar=t01[:, 1:2], in1=tmp[:, :], op0=ALU.mult, op1=ALU.add))
            done(nc.vector.tensor_tensor(tmp[:, :], tmp2[:, :], y[:, :], ALU.mult))
            done(nc.vector.tensor_scalar(d2[:, :], tmp[:, :], 1.0, None, ALU.add))
            nc.vector.tensor_copy(tmp[:, :], d2[:, :]).then_inc(d2_ready, 1)
            dve.wait_ge(rooted, 2)
            dve.wait_ge(d2_ready, 1)
            inverse_root(c, d2)
            done(nc.vector.tensor_tensor(c[:, :], c[:, :], y[:, :], ALU.mult))
            nc.vector.tensor_tensor(dc[:, :], c[:, :], d[:, :], ALU.mult).then_inc(col_ready, 1)
            dve.wait_ge(vec_spread[2], 16)
            dve.wait_ge(col_ready, 3)

            def find_and_add(s, r, t, added=None):
                last = isinstance(t, int) and t == T - 1
                if last:
                    dve.wait_ge(last_made, 1)
                else:
                    dve.wait_ge(b_out, t + 1)
                first = isinstance(t, int) and t < 2
                if not first:
                    dve.wait_ge(idx_ready, t - 1)
                nc.vector.tensor_tensor(G[s], ps[1][:, :] if last else G[s] if first else tile_of(A, t), vec[:, :], ALU.mult).then_inc(g_scaled, 1)
                if added is not None:
                    pair_rows(*added)
                dve.wait_ge(g_scaled, t + 1)
                diagonal = G[s].rearrange("p (k o) -> p k o", o=T)[:, :, bass.ds(t, 1)].rearrange("p k o -> p (k o)")
                nc.vector.scalar_tensor_tensor(out=diagonal, in0=ident[:, :], scalar=dc[:, bass.ds(t, 1)], in1=diagonal,
                                               op0=ALU.mult, op1=ALU.add).then_inc(g_ready, 1)
                if added is None:
                    dve.wait_ge(g_ready, t + 1)
                else:
                    sum_rows(*added, g_tile=t)
                nc.vector.max(out=top[r][:, :], in_=G[s]).then_inc(top_ready, 1)
                if added is not None:
                    add_rows(*added)
                dve.wait_ge(top_ready, t + 1)
                nc.vector.tensor_scalar(coef[r][:, :], top[r][:, :], c[:, bass.ds(t, 1)], None, ALU.mult).then_inc(coef_ready, 1)
                nc.vector.max_index(out=idx[r][:, :], in_max=top[r][:, :], in_values=G[s]).then_inc(idx_ready, 1)

            def pair_rows(q, t):
                dve.wait_ge(weighted, t + 1)
                nc.vector.tensor_tensor(picked[q][:, 0:2, :], picked[q][:, 0:2, :], picked[q][:, 2:4, :], ALU.add).then_inc(pairs, 1)

            def sum_rows(q, t, g_tile=None):
                dve.wait_ge(pairs, t + 1)
                if g_tile is not None:
                    dve.wait_ge(g_ready, g_tile + 1)
                nc.vector.tensor_tensor(picked[q][:, 0, :], picked[q][:, 0, :], picked[q][:, 1, :], ALU.add).then_inc(summed, 1)

            def add_rows(q, t):
                dve.wait_ge(summed, t + 1)
                nc.vector.tensor_tensor(tile_of(hs, t), tile_of(hs, t), picked[q][:, 0, :], ALU.add).then_inc(hs_ready, 1)

            for t in range(LAG):
                find_and_add(t % 2, t, t)
            with dve.Fori(0, (T - 4) // PICKS) as i:
                for j in range(PICKS):
                    t = 4 * i + j + LAG
                    find_and_add((j + LAG) % 2, (j + LAG) % PICKS, t, (j, 4 * i + j))
            find_and_add((T - 1) % 2, (T - 1) % PICKS, T - 1, ((T - 4) % PICKS, T - 4))

            def add_picked(t):
                pair_rows(t % PICKS, t)
                sum_rows(t % PICKS, t)
                add_rows(t % PICKS, t)

            for t in range(T - 3, T - 1):
                add_picked(t)

            def layer_norm(n, first, last):
                tiles = slice(first, last)
                many = last - first
                done(nc.vector.tensor_reduce(mean[:, tiles], hs[:, tiles, :], AX.X, ALU.add))
                done(nc.vector.tensor_scalar(mean[:, tiles], mean[:, tiles], 1.0 / D, None, ALU.mult))
                done(nc.vector.tensor_tensor(hs[:, tiles, :], hs[:, tiles, :], mean[:, tiles, None].to_broadcast([P, many, D]), ALU.subtract))
                done(nc.vector.tensor_tensor(sq[:, tiles, :], hs[:, tiles, :], hs[:, tiles, :], ALU.mult))
                done(nc.vector.tensor_reduce(var[:, tiles], sq[:, tiles, :], AX.X, ALU.add))
                nc.vector.tensor_scalar(var[:, tiles], var[:, tiles], 1.0 / D, EPS, ALU.mult, ALU.add).then_inc(ln_var, 1)
                dve.wait_ge(ln_root, n + 1)
                done(nc.vector.reciprocal(rstd[:, tiles], std[:, tiles]))
                nc.vector.tensor_tensor(hs[:, tiles, :], hs[:, tiles, :], rstd[:, tiles, None].to_broadcast([P, many, D]), ALU.mult).then_inc(finished, 1)

            dve.wait_ge(hs_ready, T - 1)
            dve.wait_ge(b_out, T - 1)
            layer_norm(0, 0, T - 1)
            add_picked(T - 1)
            dve.wait_ge(hs_ready, T)
            layer_norm(1, T - 1, T)

        @block.gpsimd
        def _(pool):
            made = [0]

            def const(ins):
                made[0] += 1
                ins.then_inc(making, 1)
                pool.wait_ge(making, made[0])

            def keep(buffer, pattern, base, per_partition, compare=ALU.is_ge):
                const(nc.gpsimd.affine_select(out=buffer, in_=buffer, compare_op=compare, fill=0.0, base=base,
                                              pattern=pattern, channel_multiplier=per_partition))

            const(nc.gpsimd.memset(ones[:, :], 1.0))
            const(nc.gpsimd.memset(ones_b[:, :], 1.0))
            nc.gpsimd.affine_select(out=ident[:, :], in_=ones[:, :], compare_op=ALU.is_equal, fill=0.0, base=0,
                                    pattern=[[-1, P]], channel_multiplier=1).then_inc(consts, 1)
            const(nc.gpsimd.memset(not_own, 1.0))
            keep(not_own, [[1, T], [-1, T]], 0, 0, ALU.not_equal)
            const(nc.gpsimd.memset(before, 1.0))
            keep(before, [[1, P]], -1, -1)
            keep(before, [[-T, HALF], [0, T]], 0, 1)
            const(nc.gpsimd.memset(par4[:, :, :], 1.0))
            keep(par4[:, :, :], [[-T, 2], [-2 * T, 4]], 0, 1)
            keep(par4[:, :, :], [[T, 2], [2 * T, 4]], T - 1, -1)
            const(nc.gpsimd.tensor_tensor(par4[:, :, 0:2], par4[:, :, 0:2], par4[:, :, 2:4], ALU.add))
            const(nc.gpsimd.tensor_tensor(parity[:, :], par4[:, :, 0], par4[:, :, 1], ALU.add))
            exact = dict(allow_small_or_imprecise_dtypes=True)
            const(nc.gpsimd.iota(slot_no, [[1, SLOTS]], base=0, channel_multiplier=0, **exact))
            const(nc.gpsimd.iota(my_slot[:, :], [[0, T], [P, LISTS]], base=0, channel_multiplier=1, **exact))
            const(nc.gpsimd.iota(tile_base[:, :], [[0, 2], [T, HALF], [0, LISTS]], base=0, channel_multiplier=0, **exact))
            const(nc.gpsimd.iota(tile_row[:, :], [[N, T], [0, LISTS]], base=1, channel_multiplier=0, **exact))
            const(nc.gpsimd.memset(zero_row, 0.0))
            nc.gpsimd.iota(part_no[:, :], [[0, 1]], base=0, channel_multiplier=1, **exact).then_inc(consts, 1)
            pool.dma_start(at_dram[0:1, :], zero_row).then_inc(zero_stored, 16)
            pool.wait_ge(xw_out, 1)
            pool.wait_ge(resident, T - 2)
            pool.dma_start(xw_dram.rearrange("(p t) f -> p t f", t=T), xw).then_inc(xw_stored, 16)
            pool.wait_ge(t01_ready, 1)
            nc.gpsimd.tensor_tensor(t0_ident[:, :], ident[:, :], t01[:, 0:1].to_broadcast([P, P]), ALU.mult).then_inc(making, 1)
            pool.wait_ge(making, made[0] + 1)
            steps = [0]

            def done(ins):
                steps[0] += 1
                ins.then_inc(listing, 1)
                pool.wait_ge(listing, steps[0])

            pool.wait_ge(local_ready, 1)
            done(nc.gpsimd.tensor_tensor(looked[:, :, 1], looked[:, :, 1], tile_base[:, :], ALU.subtract))

            def make_lists(h):
                half = slice(h * T, (h + 1) * T)
                tiles = slice(h * HALF, (h + 1) * HALF)
                steps[0] = 1 + 5 * h
                pool.wait_ge(counted, (h + 1) * T)
                done(nc.gpsimd.tensor_scalar(node[:, half], signs[:, half], T / 2.0, T * P / 2.0, ALU.mult, ALU.add))
                done(nc.gpsimd.tensor_tensor(node[:, half], node[:, half], looked[:, half, 1], ALU.add))
                done(nc.gpsimd.tensor_tensor(node_at[:, half], node[:, half], tile_row[:, half], ALU.add))
                done(nc.gpsimd.tensor_tensor(node_at[:, half], node_at[:, half], looked[:, half, 2], ALU.mult))
                done(nc.gpsimd.tensor_tensor(node[:, half], node[:, half], looked[:, half, 2], ALU.mult))
                nc.gpsimd.tensor_copy(lists[:, tiles, 0, :], node[:, half].rearrange("p (t q) -> p t q", t=HALF))
                nc.gpsimd.tensor_copy(lists[:, tiles, 1, :], node_at[:, half].rearrange("p (t q) -> p t q", t=HALF)).then_inc(lists_ready, 1)
                pool.wait_ge(lists_ready, h + 1)

            pool.wait_ge(resident, T)
            pool.wait_ge(col_summed, T)
            make_lists(0)

            def gather(s, t):
                if not (isinstance(t, int) and t < 2):
                    pool.wait_ge(b_made, t - 1)
                nc.gpsimd.tensor_copy(list_now[s][:, :, :].rearrange("p a q -> p (a q)"),
                                      lists[:, bass.ds(t, 1), :, :].rearrange("p o a q -> p (o a q)")).then_inc(list_taken, 1)
                pool.wait_ge(zero_stored, 16)
                early = isinstance(t, int) and t < 2
                if early:
                    wait_stored(pool, t)
                else:
                    wait_all_stored(pool)
                pool.wait_ge(list_taken, t + 1)
                pool.nop(nofuse=True)
                for q in range(LISTS):
                    pool.indirect_dma_start(out=edge[s][:, q, :], out_offset=None, in_=at_dram[0:1 + N * (t + 1 if early else T), :],
                                            in_offset=bass.IndirectOffsetOnAxis(ap=list_now[s][:, 1, q:q + 1], axis=0)).then_inc(edges_in[s], 16)

                def rows_of(q):
                    pool.indirect_dma_start(out=rows[s][q][:, :], out_offset=None, in_=adj,
                                            in_offset=bass.IndirectOffsetOnAxis(ap=list_now[s][:, 0, q:q + 1], axis=0)).then_inc(rows_in[s][q], 16)

                if isinstance(t, int) and t in (1, AHEAD):
                    pool.wait_ge(vec_stored[1 if t == 1 else 2], 16)
                    pool.nop(nofuse=True)
                rows_of(0)
                if not (early and s == 1):
                    rows_of(1)
                pool.wait_ge(own_scaled, t + 1)
                nc.gpsimd.tensor_tensor(own[s][:, :], own_raw[s][:, :], t0_ident[:, :], ALU.add).then_inc(own_ready, 1)
                if early and s == 1:
                    wait_free(pool, 2)
                    pool.nop(nofuse=True)
                    rows_of(1)

            def pick(r, t):
                if not (isinstance(t, int) and t < PICKS):
                    pool.wait_ge(hs_ready, t - PICKS + 1)
                pool.wait_ge(xw_stored, 16)
                pool.wait_ge(idx_ready, t + 1)
                pool.nop(nofuse=True)
                for m in range(TOPK):
                    pool.indirect_dma_start(out=picked[r][:, m, :], out_offset=None, in_=xw_dram,
                                            in_offset=bass.IndirectOffsetOnAxis(ap=idx[r][:, m:m + 1], axis=0)).then_inc(picks_in[r], 16)

            def weigh_all(s, n, t):
                pool.wait_ge(all_in[s], 16 * n + 16)
                nc.gpsimd.tensor_tensor(all_edges[s], all_edges[s], w[:, :, None].to_broadcast([P, T, P]), ALU.mult).then_inc(all_scaled, 1)
                pool.wait_ge(all_scaled, t + 1)
                nc.gpsimd.tensor_tensor(tile_of(all_edges[s], t), tile_of(all_edges[s], t), t0_ident[:, :], ALU.add).then_inc(all_ready, 1)

            overflow = overflow_flag(pool)
            with pool.If(overflow == 0):
                gather(0, 0)
                make_lists(1)
                for t in range(1, AHEAD):
                    gather(t % 2, t)
                for t in range(PICKS):
                    gather(t % 2, t + AHEAD)
                    pick(t, t)
                with pool.Fori(1, T // PICKS - 1) as i:
                    for j in range(PICKS):
                        gather(j % 2, PICKS * i + j + AHEAD)
                        pick(j, PICKS * i + j)
                for t in range(T - AHEAD, T):
                    pick(t % PICKS, t)
            with pool.Else():
                make_lists(1)
                for t in range(2):
                    weigh_all(t, 0, t)
                with pool.Fori(1, T // 2) as i:
                    for s in range(2):
                        weigh_all(s, i, 2 * i + s)
                for t in range(PICKS):
                    pick(t, t)
                with pool.Fori(1, T // PICKS) as i:
                    for j in range(PICKS):
                        pick(j, PICKS * i + j)


_INS = ["x", "adj", "L0_gnn_theta", "L0_gnn_W", "L0_gnn_b"]


def kernel(**inputs):
    import numpy as _np
    import concourse.bacc as _bacc
    from concourse import mybir as _mybir
    from concourse.bass_utils import run_bass_kernel_spmd as _run

    nc = _bacc.Bacc("TRN2", target_bir_lowering=False, num_devices=1)
    arrays, args = {}, []
    for name in _INS:
        a = _np.ascontiguousarray(inputs[name])
        arrays[f"in_{name}_dram"] = a
        args.append(nc.dram_tensor(f"in_{name}_dram", a.shape, _mybir.dt.from_np(a.dtype), kind="ExternalInput").ap())
    out = nc.dram_tensor("out_0_dram", inputs["x"].shape, _mybir.dt.float32, kind="ExternalOutput").ap()
    adjacency_resnorm(nc, *args, out)
    r = _run(nc, [arrays], core_ids=[0])
    return r.results[0]["out_0_dram"]
```
